# Optimizing a Trainium2 kernel written in Bass

```python
import numpy as np
import jax
import jax.numpy as jnp

def _softmax(x, axis=-1):
    return jax.nn.softmax(x, axis=axis)

def _gelu(x):
    return jax.nn.gelu(x, approximate=True)

def _silu(x):
    return jax.nn.silu(x)

def _sigmoid(x):
    return jax.nn.sigmoid(x)

def _layernorm(x, axis=-1, eps=1e-05):
    m = jnp.mean(x, axis=axis, keepdims=True)
    v = jnp.var(x, axis=axis, keepdims=True)
    return (x - m) / jnp.sqrt(v + eps)

def _scatter_add(tgt, idx, src, axis=0):
    return tgt.at[idx].add(src)

def _segment_sum(src, seg, n):
    return jax.ops.segment_sum(src, seg, n)
kernel_name = 'mk_adaln_attn_ffn_d1_seqx_r8_cf1615'

def setup_inputs(seed: int=0):
    np.random.seed(seed)
    _w = jnp.asarray

    def _rec_inputs():
        import jax
        import jax.numpy as jnp
        _rk = jax.random.key(seed)
        x = -7.109e-05 + 0.9999 * jax.random.normal(jax.random.fold_in(_rk, 1), (128, 32, 512), jnp.float32)
        _lenS = 32 - jax.random.randint(jax.random.fold_in(_rk, 7), (128,), 0, max(1, 32 // 4) + 1, jnp.int32)
        _lenS2 = 32 - jax.random.randint(jax.random.fold_in(_rk, 8), (128,), 0, max(1, 32 // 4) + 1, jnp.int32)
        itok_B_1_14 = jax.random.randint(jax.random.fold_in(_rk, 11), (128,), 1, 15, jnp.int32)
        itok_B_0_15 = jax.random.randint(jax.random.fold_in(_rk, 12), (128,), 0, 16, jnp.int32)
        return (x, itok_B_1_14, itok_B_0_15)
    x, itok_B_1_14, itok_B_0_15 = _rec_inputs()

    def _L0_cond_setup():
        import jax, jax.numpy as jnp
        import numpy as np
        B, S, D_IN = (8, 256, 512)
        A, D_OUT = (16, 512)
        key = jax.random.key(seed)
        k1, k2, k3 = jax.random.split(key, 3)
        x = jax.random.normal(k1, (B, S, D_IN), dtype=jnp.float32)
        weight = jax.random.normal(k2, (A, D_OUT, D_IN), dtype=jnp.float32) * 0.02
        adapter_ids = jax.random.randint(k3, (B,), 0, A, dtype=jnp.int64)
        return {'x': x, 'weight': weight, 'adapter_ids': adapter_ids}
    _L0_cond_all = _L0_cond_setup()
    _L0_cond_in = {k: v for k, v in _L0_cond_all.items() if k in ('weight',)}
    del _L0_cond_all

    def _L0_attn_setup():
        import jax, jax.numpy as jnp
        import numpy as np
        import math
        B, T, D_IN, D_OUT = (2, 256, 512, 512)
        N_HEADS, N_KV = (32, 8)
        HEAD_DIM = D_OUT // N_HEADS
        GROUP_SIZE = N_HEADS // N_KV
        ROPE_BASE = 500000.0
        CTX = 256

        def _rope_tables(head_dim, base, seq_len):
            inv_freq = 1.0 / base ** (jnp.arange(0, head_dim, 2, dtype=jnp.float32) / head_dim)
            t = jnp.arange(seq_len, dtype=jnp.float32)
            freqs = jnp.einsum('i,j->ij', t, inv_freq)
            return (jnp.cos(freqs), jnp.sin(freqs))

        def _apply_rope(x, cos, sin):
            x1, x2 = jnp.split(x, 2, axis=-1)
            c = cos[None, None]
            s = sin[None, None]
            return jnp.concatenate([x1 * c - x2 * s, x1 * s + x2 * c], axis=-1)
        key = jax.random.key(seed)
        ks = jax.random.split(key, 5)
        scale = 0.02
        return {'x': jax.random.normal(ks[0], (B, T, D_IN), dtype=jnp.float32), 'Wq': jax.random.normal(ks[1], (D_IN, D_OUT), dtype=jnp.float32) * scale, 'Wk': jax.random.normal(ks[2], (D_IN, N_KV * HEAD_DIM), dtype=jnp.float32) * scale, 'Wv': jax.random.normal(ks[3], (D_IN, N_KV * HEAD_DIM), dtype=jnp.float32) * scale, 'Wo': jax.random.normal(ks[4], (D_OUT, D_OUT), dtype=jnp.float32) * scale}
    _L0_attn_all = _L0_attn_setup()
    _L0_attn_in = {k: v for k, v in _L0_attn_all.items() if k in ('Wq', 'Wk', 'Wv', 'Wo')}
    del _L0_attn_all

    def _L0_cond2_setup():
        import jax, jax.numpy as jnp
        import numpy as np
        B, C, T = (64, 32, 512)
        S, D = (16, 32)
        key = jax.random.key(seed)
        k1, k2, k3 = jax.random.split(key, 3)
        x = jax.random.normal(k1, (B, C, T), dtype=jnp.float32)
        condition = jax.random.randint(k2, (B,), 0, S, dtype=jnp.int64)
        bound = float(np.sqrt(6.0 / C))
        weights = jax.random.uniform(k3, (S, C, D), dtype=jnp.float32, minval=-bound, maxval=bound)
        return {'x': x, 'condition': condition, 'weights': weights}
    _L0_cond2_all = _L0_cond2_setup()
    _L0_cond2_in = {k: v for k, v in _L0_cond2_all.items() if k in ('weights',)}
    del _L0_cond2_all

    def _L0_ffn_setup():
        import jax, jax.numpy as jnp
        import numpy as np
        BATCH, TOK, DIM, OUT = (4, 256, 512, 512)
        E, R, TOP_K = (8, 16, 2)
        SCALING = 16.0 / R
        key = jax.random.key(seed)
        ks = jax.random.split(key, 6)
        return {'x': jax.random.normal(ks[0], (BATCH, TOK, DIM), dtype=jnp.float32), 'W_base': jax.random.normal(ks[1], (OUT, DIM), dtype=jnp.float32) / np.sqrt(DIM), 'b_base': jax.random.normal(ks[2], (OUT,), dtype=jnp.float32) * 0.01, 'W_gate': jax.random.normal(ks[3], (E, DIM), dtype=jnp.float32) * 0.01, 'A': jax.random.normal(ks[4], (E, R, DIM), dtype=jnp.float32) / np.sqrt(DIM), 'B': jax.random.normal(ks[5], (OUT, OUT // OUT * R * 0 + R), dtype=jnp.float32)[None].repeat(E, 0) * 0.0 + jax.random.normal(ks[5], (E, OUT, R), dtype=jnp.float32) * 0.02}
    _L0_ffn_all = _L0_ffn_setup()
    _L0_ffn_in = {k: v for k, v in _L0_ffn_all.items() if k in ('W_base', 'b_base', 'W_gate', 'A', 'B')}
    del _L0_ffn_all
    return {'x': x, 'itok_B_1_14': itok_B_1_14, 'itok_B_0_15': itok_B_0_15, 'L0_cond_weight': _L0_cond_in['weight'], 'L0_attn_Wq': _L0_attn_in['Wq'], 'L0_attn_Wk': _L0_attn_in['Wk'], 'L0_attn_Wv': _L0_attn_in['Wv'], 'L0_attn_Wo': _L0_attn_in['Wo'], 'L0_cond2_weights': _L0_cond2_in['weights'], 'L0_ffn_W_base': _L0_ffn_in['W_base'], 'L0_ffn_b_base': _L0_ffn_in['b_base'], 'L0_ffn_W_gate': _L0_ffn_in['W_gate'], 'L0_ffn_A': _L0_ffn_in['A'], 'L0_ffn_B': _L0_ffn_in['B']}

def reference(x, itok_B_1_14, itok_B_0_15, L0_cond_weight, L0_attn_Wq, L0_attn_Wk, L0_attn_Wv, L0_attn_Wo, L0_cond2_weights, L0_ffn_W_base, L0_ffn_b_base, L0_ffn_W_gate, L0_ffn_A, L0_ffn_B):
    import jax
    import jax.numpy as jnp

    def _L0_cond_ref(x, weight, adapter_ids):
        import jax, jax.numpy as jnp
        import numpy as np
        B, S, D_IN = (8, 256, 512)
        A, D_OUT = (16, 512)
        w = weight[adapter_ids]
        return jnp.einsum('bij,bkj->bik', x, w)

    def _L0_attn_ref(x, Wq, Wk, Wv, Wo):
        import jax, jax.numpy as jnp
        import numpy as np
        import math
        B, T, D_IN, D_OUT = (2, 256, 512, 512)
        N_HEADS, N_KV = (32, 8)
        HEAD_DIM = D_OUT // N_HEADS
        GROUP_SIZE = N_HEADS // N_KV
        ROPE_BASE = 500000.0
        CTX = 256

        def _rope_tables(head_dim, base, seq_len):
            inv_freq = 1.0 / base ** (jnp.arange(0, head_dim, 2, dtype=jnp.float32) / head_dim)
            t = jnp.arange(seq_len, dtype=jnp.float32)
            freqs = jnp.einsum('i,j->ij', t, inv_freq)
            return (jnp.cos(freqs), jnp.sin(freqs))

        def _apply_rope(x, cos, sin):
            x1, x2 = jnp.split(x, 2, axis=-1)
            c = cos[None, None]
            s = sin[None, None]
            return jnp.concatenate([x1 * c - x2 * s, x1 * s + x2 * c], axis=-1)
        b, t, _ = x.shape
        cos, sin = _rope_tables(HEAD_DIM, ROPE_BASE, t)
        q = (x @ Wq).reshape(b, t, N_HEADS, HEAD_DIM).transpose(0, 2, 1, 3)
        k = (x @ Wk).reshape(b, t, N_KV, HEAD_DIM).transpose(0, 2, 1, 3)
        v = (x @ Wv).reshape(b, t, N_KV, HEAD_DIM).transpose(0, 2, 1, 3)
        q = _apply_rope(q, cos, sin)
        k = _apply_rope(k, cos, sin)
        k_h = jnp.repeat(k, GROUP_SIZE, axis=1)
        v_h = jnp.repeat(v, GROUP_SIZE, axis=1)
        scores = jnp.einsum('bhqd,bhkd->bhqk', q, k_h) / math.sqrt(HEAD_DIM)
        causal = jnp.triu(jnp.ones((t, t), dtype=bool), k=1)
        scores = jnp.where(causal[None, None], jnp.finfo(scores.dtype).min, scores)
        attn = jax.nn.softmax(scores, axis=-1)
        ctx = jnp.einsum('bhqk,bhkd->bhqd', attn, v_h)
        ctx = ctx.transpose(0, 2, 1, 3).reshape(b, t, D_OUT)
        return ctx @ Wo

    def _L0_cond2_ref(x, condition, weights):
        import jax, jax.numpy as jnp
        import numpy as np
        B, C, T = (64, 32, 512)
        S, D = (16, 32)
        W = weights[condition]
        return jnp.einsum('bct,bcd->bdt', x, W)

    def _L0_ffn_ref(x, W_base, b_base, W_gate, A, B):
        import jax, jax.numpy as jnp
        import numpy as np
        BATCH, TOK, DIM, OUT = (4, 256, 512, 512)
        E, R, TOP_K = (8, 16, 2)
        SCALING = 16.0 / R
        result = jnp.einsum('bnd,od->bno', x, W_base) + b_base
        logits = jnp.einsum('bnd,ed->bne', x, W_gate)
        probs = jax.nn.softmax(logits.astype(jnp.float32), axis=-1)
        top_p, top_i = jax.lax.top_k(probs, TOP_K)
        top_p = top_p / jnp.sum(top_p, axis=-1, keepdims=True)
        top_p = top_p.astype(x.dtype)
        route_w = jnp.sum(jax.nn.one_hot(top_i, E, dtype=x.dtype) * top_p[..., None], axis=-2)
        h = jnp.einsum('bnd,erd->bner', x, A)
        hw = h * route_w[..., None]
        delta = jnp.einsum('bner,eor->bno', hw, B)
        return result + delta * SCALING
    x = x + _L0_attn_ref(_L0_cond_ref(x, L0_cond_weight, itok_B_1_14), L0_attn_Wq, L0_attn_Wk, L0_attn_Wv, L0_attn_Wo)
    x = x + _L0_ffn_ref(_L0_cond2_ref(x, itok_B_0_15, L0_cond2_weights), L0_ffn_W_base, L0_ffn_b_base, L0_ffn_W_gate, L0_ffn_A, L0_ffn_B)
    return x

_drawn_inputs = setup_inputs


def setup_inputs(seed=0):
    import zlib

    import numpy as np

    out = dict(_drawn_inputs(seed))
    spreads = {}
    factors = {'L0_attn_Wq': 8.0, 'L0_attn_Wk': 8.0, 'L0_ffn_b_base': 8.0}
    for name, (base, spread) in spreads.items():
        noise = np.random.default_rng([zlib.crc32(name.encode()), seed]).standard_normal(out[name].shape)
        drawn = base * np.exp(spread * noise) if base else spread * noise
        out[name] = jnp.asarray(drawn.astype(out[name].dtype))
    for name, factor in factors.items():
        out[name] = (out[name] * factor).astype(out[name].dtype)
    return out
```

```python
from contextlib import ExitStack

import numpy as np

import concourse.bass as bass
from concourse import mybir

F32 = mybir.dt.float32
F32R = mybir.dt.float32r
BF16 = mybir.dt.bfloat16
I32 = mybir.dt.int32
ALU = mybir.AluOpType
ACT = mybir.ActivationFunctionType
X = mybir.AxisListType.X

P = 128
NB, T, D = 128, 32, 512
KC = D // P
NA = 16
SPT = P // T
NT = NB // SPT
ST = (NB + NA * (SPT - 1)) // SPT
NSLOT = ST * SPT
KV, G, HD = 8, 4, 16
HALF = HD // 2
NQ, NKV = KV * G * HD, KV * HD
NQK = NQ + NKV
NQKV = NQ + 2 * NKV
E, R = 8, 16
ER = E * R
NF = D + ER + E
VW = HD + 1
XB = 4
NEG = -1.0e30
ROPE_BASE = 500000.0


def constants():
    p = np.arange(P)
    slot = np.arange(NSLOT)
    inv = (1.0 / ROPE_BASE ** (np.arange(0, HD, 2, dtype=np.float32) / HD)).astype(np.float32)
    angle = ((p % T).astype(np.float32)[:, None] * inv[None, :]).astype(np.float32)
    cos, sin = np.cos(angle), np.sin(angle)
    rows = np.ones((P, 1))
    a = np.arange(NA)
    parts = {
        "ident": np.eye(P),
        "cos": np.concatenate([cos, cos], 1),
        "sin": np.concatenate([-sin, sin], 1),
        "kvmask": (p[:, None] // HD == np.arange(KV)[None, :]),
        "own_sample": (p[:, None] // T == np.arange(SPT)[None, :]),
        "before": (p[:, None] < p[None, :]),
        "ones": np.ones((P, P)),
        "causal": np.where(np.arange(T)[None, :] > (p % T)[:, None], NEG, 0.0),
        "iota_a": rows * a,
        "rev_e": rows * (E - np.arange(E)),
        "four_m": rows * (SPT * np.arange(NB // SPT)),
        "upto": rows * (a[None, :] <= a[:, None]).reshape(1, -1),
        "iota_slot": rows * slot,
        "iota_tile": rows * np.arange(ST),
        "sample": p[:, None],
        "pad_place": rows * (NB + slot),
    }
    at, where = 0, {}
    for name, v in parts.items():
        where[name] = (at, v.shape[1])
        at += v.shape[1]
    return np.ascontiguousarray(np.concatenate([np.asarray(v, np.float32) for v in parts.values()], 1)), where


def build(nc, x, xt, ids_a, ids_m, wcond, wqkv, wo, wmix, wffn, wb, bias, consts, out, where):
    ncols = consts.shape[1]
    with ExitStack() as ctx:
        def sb(name, shape, dt=F32):
            return ctx.enter_context(nc.sbuf_tensor(name, shape, dt))

        def sem(name):
            return ctx.enter_context(nc.semaphore(name))

        ps = ctx.enter_context(nc.psum_tensor("ps", [P, 8, 512], F32))
        y_rows = nc.dram_tensor("y_rows", ((NB + NSLOT) * T, D), F32, kind="Internal").ap()

        cst = sb("cst", [P, ncols])

        def const(name):
            a, n = where[name]
            return cst[:, a:a + n]

        ident = const("ident")
        ident_bf = sb("ident_bf", [P, P], BF16)
        causal_bf = sb("causal_bf", [P, 2 * KV * T], BF16)
        wqkv_h = sb("wqkv_h", [P, KC, NQKV], F32R)
        wqkv_l = sb("wqkv_l", [P, KC, NQKV], F32R)
        mix_bd = sb("mix_bd", [P, NT, P])

        stage1 = ExitStack()
        def sb1(name, shape, dt=F32):
            return stage1.enter_context(nc.sbuf_tensor(name, shape, dt))
        w_all = sb1("w_all", [P, NA, KC, D])
        xt_raw = [sb1(f"xt_raw{u}", [P, SPT, KC, T]) for u in range(XB)]
        xt_sb = [sb1(f"xt_sb{p}", [P, KC, SPT, T]) for p in range(2)]
        y_sb = [sb1(f"y_sb{u}", [P, D]) for u in range(2)]
        wqkv_raw = sb1("wqkv_raw", [P, KC, NQKV])
        wide = sb1("wide", [P, ST * NA])
        ids_col = sb1("ids_col", [P, 1], I32)
        idsm_row = sb1("idsm_row", [1, NB], I32)
        idsf = sb1("idsf", [P, 1])
        onehot = sb1("onehot", [P, NA])
        tiles_a = sb1("tiles_a", [P, NA])
        end_a = sb1("end_a", [P, NA])
        base_a = sb1("base_a", [P, NA])
        pos_a = sb1("pos_a", [P, NA])
        pos = sb1("pos", [P, 1])
        match = wide[:, 0:NSLOT]
        adapter_f = sb1("adapter_f", [P, ST])
        tile_adapter = sb1("tile_adapter", [P, ST], I32)
        slot_sample = sb1("slot_sample", [1, NSLOT], I32)
        pad = wide[0:1, NSLOT:2 * NSLOT]
        slot_store = sb1("slot_store", [1, NSLOT], I32)
        stage1.close()

        y_nat = [sb(f"y_nat{p}", [P, D]) for p in range(2)]
        x_nat = [sb(f"x_nat{p}", [P, D]) for p in range(2)]
        yt_h = sb("yt_h", [P, KC, P], F32R)
        yt_l = sb("yt_l", [P, KC, P], F32R)
        rope_a = sb("rope_a", [P, NQK])
        rope_b = sb("rope_b", [P, NQK])
        qk = sb("qk", [P, NQK])
        v_bd = [sb(f"v_bd{p}", [P, KV, SPT, VW]) for p in range(2)]
        qt = sb("qt", [P, SPT, P])
        k_bd = sb("k_bd", [P, SPT, KV, T])
        row_max = sb("row_max", [P, SPT * KV])
        prob = sb("prob", [P, KV, SPT, T])
        pt = sb("pt", [P, KV, P])
        recip = sb("recip", [P, KV, SPT])
        cx = sb("cx", [P, SPT, KV, HD])
        cxt_h = sb("cxt_h", [P, G, SPT, T], F32R)
        cxt_l = sb("cxt_l", [P, G, SPT, T], F32R)
        x2 = sb("x2", [P, D])
        x2b = [sb(f"x2b{p}", [P, D]) for p in range(2)]
        x3t_h = sb("x3t_h", [P, KC, P], F32R)
        x3t_l = sb("x3t_l", [P, KC, P], F32R)
        logit = sb("logit", [P, E])
        logit2 = sb("logit2", [P, E])
        first = sb("first", [P, E])
        second = sb("second", [P, E])
        pick = sb("pick", [P, E])
        route = sb("route", [P, E])
        rs = sb("rs", [P, 8])
        hw = sb("hw", [P, E, R])
        hwt = sb("hwt", [P, P])
        o_sb = [sb(f"o_sb{p}", [P, D]) for p in range(2)]
        wo_raw = sb("wo_raw", [P, G, D])
        wo_h = sb("wo_h", [P, G, D], F32R)
        wo_l = sb("wo_l", [P, G, D], F32R)
        wf_raw = sb("wf_raw", [P, KC, NF])
        wf_h = sb("wf_h", [P, KC, NF], F32R)
        wf_l = sb("wf_l", [P, KC, NF], F32R)
        wb_sb = sb("wb_sb", [P, D])
        bias_sb = sb("bias_sb", [P, D])

        cst_in = sem("cst_in")
        ids_in = sem("ids_in")
        w_in = [sem(f"w_in{a}") for a in range(NA)]
        wqkv_in = sem("wqkv_in")
        xt_in = [sem(f"xt_in{u}") for u in range(XB)]
        mix_in = sem("mix_in")
        w2_in = sem("w2_in")
        y_in = [sem(f"y_in{p}") for p in range(2)]
        x_in = [sem(f"x_in{p}") for p in range(2)]
        set_up = sem("set_up")
        route_ps = sem("route_ps")
        routed = sem("routed")
        w_ready = sem("w_ready")
        xt_ready = sem("xt_ready")
        y_ps = sem("y_ps")
        y_copied = sem("y_copied")
        y_stored = [sem(f"y_stored{u}") for u in range(2)]
        zeroed = sem("zeroed")
        wqkv_hi = sem("wqkv_hi")
        wqkv_lo = sem("wqkv_lo")
        w2_hi = sem("w2_hi")
        w2_lo = sem("w2_lo")
        yt_ps, yt_hi, yt_lo = sem("yt_ps"), sem("yt_hi"), sem("yt_lo")
        qkv_ps, roped_parts, roped, v_ready = sem("qkv_ps"), sem("roped_parts"), sem("roped"), sem("v_ready")
        qkt_ps, qt_ready, k_ready = sem("qkt_ps"), sem("qt_ready"), sem("k_ready")
        scores_ps, max_ready, shifted, exp_ready = sem("scores_ps"), sem("max_ready"), sem("shifted"), sem("exp_ready")
        pt_ps, pt_lower, pt_upper = sem("pt_ps"), sem("pt_lower"), sem("pt_upper")
        cx_ps, recip_ready, cx_ready = sem("cx_ps"), sem("recip_ready"), sem("cx_ready")
        cxt_ps, cxt_hi, cxt_lo = sem("cxt_ps"), sem("cxt_hi"), sem("cxt_lo")
        wo_ps, x2_ready, x2b_ready = sem("wo_ps"), sem("x2_ready"), sem("x2b_ready")
        x3t_ps, x3t_hi, x3t_lo = sem("x3t_ps"), sem("x3t_hi"), sem("x3t_lo")
        h_ps, route_step, gate_exp = sem("h_ps"), sem("route_step"), sem("gate_exp")
        hw_ready, hwt_ps, hwt_ready = sem("hw_ready"), sem("hwt_ps"), sem("hwt_ready")
        out_ps, out_ready = sem("out_ps"), sem("out_ready")
        out_stored = [sem(f"out_stored{p}") for p in range(2)]

        RSTEPS = 12

        def need(eng, s, n):
            if not isinstance(n, int) or n > 0:
                eng.wait_ge(s, n)

        def has(t):
            return not isinstance(t, int) or 0 <= t < NT

        def pipelined(eng, iteration, ahead=1):
            for i in range(4):
                iteration(i, i % 2, i // 2)
            with eng.Fori(2, NT // 2 - ahead) as k:
                for u in range(2):
                    iteration(k * 2 + u, u, k)
            for i in range(NT - 2 * ahead, NT + 2):
                iteration(i, i % 2, i // 2)

        block = ctx.enter_context(nc.Block())

        @block.sync
        def _(sp):
            sp.dma_start(ids_col[:], ids_a.rearrange("(p a) -> p a", a=1)).then_inc(ids_in, 16)
            sp.dma_start(idsm_row[:], ids_m.rearrange("(a p) -> a p", a=1)).then_inc(ids_in, 16)
            sp.dma_start(cst[:], consts).then_inc(cst_in, 16)
            sp.wait_ge(routed, 1)

            def gather(i, u, again):
                regs = [sp.value_load(slot_sample[0:1, bass.ds((i * XB + u) * SPT + j, 1)], min_val=0, max_val=NB - 1)
                        for j in range(SPT)]
                for j in range(SPT):
                    if again and j == 0:
                        sp.wait_ge(xt_ready, i * XB + (u - XB + 1))
                    sp.dma_start(xt_raw[u][:, j].rearrange("p c t -> p (c t)"), xt[bass.ds(regs[j] * P, P), :]).then_inc(xt_in[u], 16)

            for u in range(XB):
                gather(0, u, False)
            with sp.Fori(1, ST // XB) as i:
                for u in range(XB):
                    gather(i, u, True)

            sp.wait_ge(y_ps, ST)
            sp.wait_ge(y_copied, ST)
            sp.wait_ge(mix_in, 16 * NB)
            sp.wait_ge(wqkv_lo, 1)
            for u in range(2):
                sp.wait_ge(y_stored[u], 64 * (ST // 2))

            def rows(t):
                return bass.ds(t * P, P)

            def load_y(t, p):
                if has(t):
                    need(sp, yt_ps, t - 1)
                    sp.dma_start(y_nat[p][:], y_rows[rows(t), :]).then_inc(y_in[p], 16)

            def load_x(t, p):
                if has(t):
                    need(sp, x2_ready, t - 1)
                    sp.dma_start(x_nat[p][:], x[rows(t), :]).then_inc(x_in[p], 16)

            load_y(0, 0)
            load_y(1, 1)
            load_x(0, 0)
            sp.dma_start(wo_raw[:], wo).then_inc(w2_in, 16)
            sp.dma_start(wf_raw[:], wffn).then_inc(w2_in, 16)
            sp.dma_start(wb_sb[:], wb).then_inc(w2_in, 16)
            sp.dma_start(bias_sb[:], bias.rearrange("(a d) -> a d", a=1).broadcast_to([P, D])).then_inc(w2_in, 16)
            load_y(2, 0)

            def iteration(i, p, k):
                load_y(i + 3, 1 - p)
                if has(i - 2):
                    sp.wait_ge(out_ready, i - 1)
                    sp.dma_start(out[rows(i - 2), :], o_sb[p][:]).then_inc(out_stored[p], 16)
                load_x(i + 1, 1 - p)

            pipelined(sp, iteration, ahead=2)
            for p in range(2):
                sp.wait_ge(out_stored[p], 16 * (NT // 2))

        @block.gpsimd
        def _(pool):
            pool.memset(mix_bd[:], 0.0).then_inc(zeroed, 1)

            pool.wait_ge(ids_in, 32)
            pool.wait_ge(zeroed, 1)
            for a in range(NA):
                if a >= 3:
                    pool.wait_ge(w_in[a - 3], 16)
                    pool.sem_inc(w_ready, 1)
                pool.dma_start(w_all[:, a], wcond[a]).then_inc(w_in[a], 16)
                with pool.Fori(a * NT // NA, (a + 1) * NT // NA) as g:
                    for j in range(SPT):
                        m = pool.value_load(idsm_row[0:1, bass.ds(g * SPT + j, 1)], min_val=0, max_val=NA - 1)
                        q = slice(j * T, (j + 1) * T)
                        pool.dma_start(mix_bd[q, bass.ds(g, 1), q], wmix[bass.ds(m * T, T), :]
                                       .rearrange("c (a d) -> c a d", a=1)).then_inc(mix_in, 16)
            pool.dma_start(wqkv_raw[:], wqkv).then_inc(wqkv_in, 16)
            for a in range(NA - 3, NA):
                pool.wait_ge(w_in[a], 16)
                pool.sem_inc(w_ready, 1)

            pool.wait_ge(y_ps, ST)
            for u in range(2):
                pool.wait_ge(y_stored[u], 64 * (ST // 2))
            pool.wait_ge(mix_in, 16 * NB)
            pool.wait_ge(wqkv_lo, 1)
            for p in range(2):
                pool.memset(v_bd[p][:], 0.0).then_inc(zeroed, 1)
            pool.wait_ge(zeroed, 3)
            for p in range(2):
                pool.tensor_copy(v_bd[p][:, :, :, HD], const("own_sample").rearrange("p (h s) -> p h s", h=1)
                                 .broadcast_to([P, KV, SPT])).then_inc(zeroed, 1)

            def iteration(i, p, k):
                if has(i):
                    pool.wait_ge(roped_parts, i + 1)
                    need(pool, qkt_ps, i)
                    pool.tensor_tensor(qk[:], rope_a[:], rope_b[:], ALU.add).then_inc(roped, 1)
                if has(i - 1):
                    if isinstance(i, int) and i == 1:
                        pool.wait_ge(w2_in, 64)
                    pool.wait_ge(x2_ready, i)
                    need(pool, out_ready, i - 2)
                    pool.tensor_tensor(x2b[1 - p][:], x2[:], bias_sb[:], ALU.add).then_inc(x2b_ready, 1)

            pipelined(pool, iteration)

        @block.scalar
        def _(act):
            def store_y(i, u):
                tile = i * XB + u
                regs = [act.value_load(slot_store[0:1, bass.ds(tile * SPT + j, 1)], min_val=0, max_val=NB + NSLOT - 1)
                        for j in range(SPT)]
                for j in range(SPT):
                    if j == 0:
                        act.wait_ge(y_copied, tile + 1)
                    act.dma_start(y_rows[bass.ds(regs[j] * T, T), :], y_sb[u % 2][j * T:(j + 1) * T, :]) \
                       .then_inc(y_stored[u % 2], 16)

            act.wait_ge(routed, 2)
            with act.Fori(0, ST // XB) as i:
                for u in range(XB):
                    store_y(i, u)
            act.wait_ge(wqkv_in, 16)
            act.activation(wqkv_h[:], wqkv_raw[:], ACT.Copy).then_inc(wqkv_hi, 1)

            act.wait_ge(y_ps, ST)
            for u in range(2):
                act.wait_ge(y_stored[u], 64 * (ST // 2))
            act.wait_ge(mix_in, 16 * NB)
            act.wait_ge(wqkv_lo, 1)

            def split_hi(t):
                if has(t):
                    act.wait_ge(yt_ps, t + 1)
                    need(act, qkv_ps, t)
                    act.activation(yt_h[:], ps[:, 0, :].rearrange("p (c n) -> p c n", c=KC), ACT.Copy).then_inc(yt_hi, 1)

            split_hi(0)

            def iteration(i, p, k):
                if has(i - 1):
                    act.wait_ge(shifted, i)
                    act.activation(prob[:], prob[:], ACT.Exp, scale=HD ** -0.5).then_inc(exp_ready, 1)
                if has(i):
                    act.wait_ge(roped_parts, i + 1)
                    if isinstance(i, int) and i == 0:
                        act.wait_ge(zeroed, 5)
                    need(act, cx_ps, i - 1)
                    for j in range(SPT):
                        q = slice(j * T, (j + 1) * T)
                        last = act.activation(v_bd[p][q, :, j, 0:HD],
                                              ps[q, 2, NKV:2 * NKV].rearrange("p (h d) -> p h d", h=KV), ACT.Copy)
                    last.then_inc(v_ready, 1)
                if has(i - 1):
                    act.wait_ge(pt_ps, i)
                    need(act, cx_ps, i - 1)
                    act.activation(pt[:, 0:KV // 2], ps[:, 3, :].rearrange("p (h n) -> p h n", h=KV // 2),
                                   ACT.Copy).then_inc(pt_lower, 1)
                split_hi(i + 1)
                if has(i - 2):
                    act.wait_ge(route_step, (i - 2) * RSTEPS + 7)
                    act.activation(rs[:, 4:5], rs[:, 0:1], ACT.Exp, bias=rs[:, 2:3], scale=-1.0).then_inc(gate_exp, 1)
                    act.wait_ge(hwt_ps, i - 1)
                    need(act, out_ps, i - 2)
                    act.activation(hwt[:], ps[:, 6, 0:P], ACT.Copy).then_inc(hwt_ready, 1)
                if has(i - 1):
                    act.wait_ge(cxt_ps, i)
                    need(act, wo_ps, i - 1)
                    act.activation(cxt_h[:].rearrange("p g s t -> p s g t"),
                                   ps[:, 0, :].rearrange("p (s g t) -> p s g t", s=SPT, g=G), ACT.Copy).then_inc(cxt_hi, 1)
                if has(i):
                    act.wait_ge(qkt_ps, i + 1)
                    need(act, scores_ps, i)
                    act.activation(qt[:].rearrange("p s (g t) -> p s g t", g=G),
                                   ps[:, 1, :].rearrange("p (g s t) -> p s g t", s=SPT, g=G), ACT.Copy).then_inc(qt_ready, 1)
                if isinstance(i, int) and i == 0:
                    act.wait_ge(w2_in, 64)
                    act.activation(wo_h[:], wo_raw[:], ACT.Copy)
                    act.activation(wf_h[:], wf_raw[:], ACT.Copy).then_inc(w2_hi, 1)
                if has(i - 1):
                    act.wait_ge(x3t_ps, i)
                    need(act, out_ps, i - 1)
                    act.activation(x3t_h[:], ps[:, 6, :].rearrange("p (c n) -> p c n", c=KC), ACT.Copy).then_inc(x3t_hi, 1)

            pipelined(act, iteration)

        @block.vector
        def _(dve):
            steps = [0]

            def then(ins):
                steps[0] += 1
                ins.then_inc(set_up, 1)
                dve.wait_ge(set_up, steps[0])

            dve.wait_ge(ids_in, 32)
            then(dve.tensor_copy(idsf[:], ids_col[:]))
            dve.wait_ge(cst_in, 16)
            then(dve.tensor_scalar(onehot[:], const("iota_a"), idsf[:, 0:1], None, ALU.is_equal))
            dve.tensor_copy(ident_bf[:], ident)
            dve.tensor_copy(causal_bf[:].rearrange("p (h t) -> p h t", t=T),
                            const("causal").rearrange("p (a t) -> p a t", a=1).broadcast_to([P, 2 * KV, T]))
            dve.wait_ge(route_ps, 1)
            wide_m = wide[:, 0:NA * NT].rearrange("p (a m) -> p a m", a=NA)
            count = ps[:, 0, NA:2 * NA].rearrange("p (a m) -> p a m", m=1).broadcast_to([P, NA, NT])
            four = const("four_m").rearrange("p (a m) -> p a m", a=1).broadcast_to([P, NA, NT])
            then(dve.tensor_tensor(wide_m, count, four, ALU.is_gt))
            then(dve.tensor_reduce(tiles_a[:], wide_m, X, ALU.add))
            wide_a = wide[:, 0:NA * NA].rearrange("p (a b) -> p a b", a=NA)
            upto = const("upto").rearrange("p (a b) -> p a b", a=NA)
            then(dve.tensor_tensor(wide_a, upto, tiles_a[:].rearrange("p (a b) -> p a b", a=1).broadcast_to([P, NA, NA]),
                                   ALU.mult))
            then(dve.tensor_reduce(end_a[:], wide_a, X, ALU.add))
            then(dve.tensor_tensor(base_a[:], end_a[:], tiles_a[:], ALU.subtract))
            then(dve.scalar_tensor_tensor(pos_a[:], base_a[:], float(SPT), ps[:, 0, 0:NA], ALU.mult, ALU.add))
            then(dve.tensor_tensor(pos_a[:], pos_a[:], onehot[:], ALU.mult))
            then(dve.tensor_reduce(pos[:], pos_a[:], X, ALU.add))
            wide_t = wide[:, 0:ST * NA].rearrange("p (t a) -> p t a", a=NA)
            tile_no = const("iota_tile").rearrange("p (t a) -> p t a", a=1).broadcast_to([P, ST, NA])
            then(dve.tensor_tensor(wide_t, tile_no, end_a[:].rearrange("p (t a) -> p t a", t=1).broadcast_to([P, ST, NA]),
                                   ALU.is_ge))
            then(dve.tensor_reduce(adapter_f[:], wide_t, X, ALU.add))
            dve.tensor_scalar(tile_adapter[:], adapter_f[:], float(NA - 1), None, ALU.min)
            then(dve.tensor_scalar(match, const("iota_slot"), pos[:, 0:1], None, ALU.is_equal))
            assert steps[0] == MATCH_STEP
            dve.wait_ge(route_ps, 2)
            dve.tensor_copy(slot_sample[:], ps[0:1, 1, 0:NSLOT]).then_inc(routed, 1)
            then(dve.tensor_scalar(pad, ps[0:1, 2, 0:NSLOT], -1.0, 1.0, ALU.mult, ALU.add))
            then(dve.tensor_tensor(pad, pad, const("pad_place")[0:1, :], ALU.mult))
            dve.tensor_tensor(slot_store[:], ps[0:1, 1, 0:NSLOT], pad, ALU.add).then_inc(routed, 1)

            def order_x(i, u, again):
                dve.wait_ge(xt_in[u], i * 64 + 64)
                if again or u >= 2:
                    dve.wait_ge(y_ps, i * XB + (u - 1))
                dve.tensor_copy(xt_sb[u % 2][:].rearrange("p c s t -> p s c t"), xt_raw[u][:]).then_inc(xt_ready, 1)

            def copy_y(i, u, again):
                dve.wait_ge(y_ps, i * XB + u + 1)
                if again or u >= 2:
                    dve.wait_ge(y_stored[u % 2], i * 128 + 64 * (u // 2))
                dve.tensor_copy(y_sb[u % 2][:], ps[:, 4 + u, :]).then_inc(y_copied, 1)

            order_x(0, 0, False)
            for u in range(XB):
                if u + 1 < XB:
                    order_x(0, u + 1, False)
                else:
                    order_x(1, 0, True)
                copy_y(0, u, False)
            with dve.Fori(1, ST // XB - 1) as i:
                for u in range(XB):
                    order_x(i if u + 1 < XB else i + 1, (u + 1) % XB, True)
                    copy_y(i, u, True)
            for u in range(XB):
                if u + 1 < XB:
                    order_x(ST // XB - 1, u + 1, True)
                copy_y(ST // XB - 1, u, True)
            dve.wait_ge(wqkv_hi, 1)
            dve.tensor_tensor(wqkv_l[:], wqkv_raw[:], wqkv_h[:].bitcast(F32), ALU.subtract).then_inc(wqkv_lo, 1)

            for u in range(2):
                dve.wait_ge(y_stored[u], 64 * (ST // 2))
            dve.wait_ge(mix_in, 16 * NB)
            dve.wait_ge(wqkv_lo, 1)

            def split_lo(t):
                if has(t):
                    dve.wait_ge(yt_hi, t + 1)
                    dve.tensor_tensor(yt_l[:], ps[:, 0, :].rearrange("p (c n) -> p c n", c=KC),
                                      yt_h[:].bitcast(F32), ALU.subtract).then_inc(yt_lo, 1)

            split_lo(0)
            cos = const("cos").rearrange("p (h d) -> p h d", h=1).broadcast_to([P, NQK // HD, HD])
            sin = [const("sin")[:, s * HALF:(s + 1) * HALF].rearrange("p (h d) -> p h d", h=1)
                   .broadcast_to([P, NQK // HD, HALF]) for s in range(2)]
            banks12 = ps[:, 1:3, :].rearrange("p a n -> p (a n)")
            qk_ps = banks12[:, 0:NQK].rearrange("p (h d) -> p h d", d=HD)
            sc = ps[:, 3:5, :].rearrange("p a n -> p (a n)").rearrange("p (h t) -> p h t", t=T)
            cxp = ps[:, 3:5, :].rearrange("p a n -> p (a n)").rearrange("p (h w) -> p h w", h=KV)[:, :, 0:SPT * VW] \
                .rearrange("p h (s w) -> p h s w", s=SPT)
            rev = const("rev_e")

            def routing(t):
                at = [0]

                def step(ins):
                    at[0] += 1
                    ins.then_inc(route_step, 1)
                    dve.wait_ge(route_step, t * RSTEPS + at[0])

                max1, key1, max2, key2, e2, den, r1, r2 = (rs[:, n:n + 1] for n in range(8))
                dve.wait_ge(h_ps, t + 1)
                step(dve.tensor_copy(logit[:], ps[:, 5, ER:ER + E]))
                step(dve.tensor_reduce(max1, logit[:], X, ALU.max))
                step(dve.scalar_tensor_tensor(pick[:], logit[:], max1, rev, ALU.is_equal, ALU.mult))
                step(dve.tensor_reduce(key1, pick[:], X, ALU.max))
                step(dve.tensor_scalar(first[:], rev, key1, None, ALU.is_equal))
                step(dve.scalar_tensor_tensor(logit2[:], first[:], 3.0 * NEG, logit[:], ALU.mult, ALU.add))
                step(dve.tensor_reduce(max2, logit2[:], X, ALU.max))
                step(dve.scalar_tensor_tensor(pick[:], logit2[:], max2, rev, ALU.is_equal, ALU.mult))
                dve.tensor_reduce(key2, pick[:], X, ALU.max)
                dve.wait_ge(gate_exp, t + 1)
                step(dve.tensor_scalar(den, e2, 1.0, None, ALU.add))
                dve.tensor_scalar(second[:], rev, key2, None, ALU.is_equal)
                step(dve.reciprocal(r1, den))
                dve.tensor_scalar(route[:], first[:], r1, None, ALU.mult)
                step(dve.tensor_tensor(r2, e2, r1, ALU.mult))
                step(dve.scalar_tensor_tensor(route[:], second[:], r2, route[:], ALU.mult, ALU.add))
                assert at[0] == RSTEPS
                need(dve, hwt_ps, t)
                dve.tensor_tensor(hw[:], ps[:, 5, 0:ER].rearrange("p (e r) -> p e r", e=E),
                                  route[:].rearrange("p (e r) -> p e r", r=1).broadcast_to([P, E, R]),
                                  ALU.mult).then_inc(hw_ready, 1)

            def iteration(i, p, k):
                if has(i - 1):
                    dve.wait_ge(scores_ps, i)
                    dve.tensor_reduce(row_max[:], sc, X, ALU.max).then_inc(max_ready, 1)
                    dve.wait_ge(max_ready, i)
                    need(dve, pt_ps, i - 1)
                    dve.tensor_tensor(prob[:].rearrange("p h s t -> p s h t"), sc.rearrange("p (s h) t -> p s h t", h=KV),
                                      row_max[:].rearrange("p (s h t) -> p s h t", h=KV, t=1)
                                      .broadcast_to([P, SPT, KV, T]), ALU.subtract).then_inc(shifted, 1)
                if has(i):
                    dve.wait_ge(qkv_ps, i + 1)
                    need(dve, roped, i)
                    dve.tensor_tensor(rope_a[:].rearrange("p (h d) -> p h d", d=HD), qk_ps, cos, ALU.mult)
                    for s in range(2):
                        last = dve.tensor_tensor(
                            rope_b[:].rearrange("p (h d) -> p h d", d=HD)[:, :, s * HALF:(s + 1) * HALF],
                            qk_ps[:, :, (1 - s) * HALF:(2 - s) * HALF], sin[s], ALU.mult)
                    last.then_inc(roped_parts, 1)
                if has(i - 1):
                    dve.wait_ge(pt_ps, i)
                    need(dve, cx_ps, i - 1)
                    dve.tensor_copy(pt[:, KV // 2:KV], ps[:, 4, :].rearrange("p (h n) -> p h n", h=KV // 2)) \
                       .then_inc(pt_upper, 1)
                split_lo(i + 1)
                if has(i - 2):
                    routing(i - 2)
                if has(i - 1):
                    dve.wait_ge(cx_ps, i)
                    dve.reciprocal(recip[:], cxp[:, :, :, HD]).then_inc(recip_ready, 1)
                    dve.wait_ge(recip_ready, i)
                    need(dve, cxt_ps, i - 1)
                    for s in range(SPT):
                        last = dve.tensor_tensor(cx[:, s], cxp[:, :, s, 0:HD],
                                                 recip[:, :, s:s + 1].broadcast_to([P, KV, HD]), ALU.mult)
                    last.then_inc(cx_ready, 1)
                    dve.wait_ge(cxt_hi, i)
                    dve.tensor_tensor(cxt_l[:].rearrange("p g s t -> p s g t"),
                                      ps[:, 0, :].rearrange("p (s g t) -> p s g t", s=SPT, g=G),
                                      cxt_h[:].bitcast(F32).rearrange("p g s t -> p s g t"), ALU.subtract).then_inc(cxt_lo, 1)
                if has(i - 2):
                    dve.wait_ge(out_ps, i - 1)
                    dve.wait_ge(x2b_ready, i - 1)
                    need(dve, out_stored[p], k * 16 - 16)
                    dve.tensor_tensor(o_sb[p][:], ps[:, 7, :], x2b[p][:], ALU.add).then_inc(out_ready, 1)
                if has(i):
                    dve.wait_ge(qkt_ps, i + 1)
                    need(dve, scores_ps, i)
                    kt = ps[:, 2, 0:P].rearrange("p (s h t) -> p s h t", s=SPT, h=1)
                    mask = const("kvmask").rearrange("p (h t) -> p h t", t=1).broadcast_to([P, KV, T])
                    for s in range(SPT):
                        last = dve.tensor_tensor(k_bd[:, s], kt[:, s].broadcast_to([P, KV, T]), mask, ALU.mult)
                    last.then_inc(k_ready, 1)
                if isinstance(i, int) and i == 0:
                    dve.wait_ge(w2_hi, 1)
                    dve.tensor_tensor(wo_l[:], wo_raw[:], wo_h[:].bitcast(F32), ALU.subtract)
                    dve.tensor_tensor(wf_l[:], wf_raw[:], wf_h[:].bitcast(F32), ALU.subtract).then_inc(w2_lo, 1)
                if has(i - 1):
                    dve.wait_ge(wo_ps, i)
                    dve.wait_ge(x_in[1 - p], k * 16 + 16 * p)
                    need(dve, x3t_ps, i - 1)
                    need(dve, x2b_ready, i - 1)
                    dve.tensor_tensor(x2[:], ps[:, 5, :], x_nat[1 - p][:], ALU.add).then_inc(x2_ready, 1)
                    dve.wait_ge(x3t_hi, i)
                    dve.tensor_tensor(x3t_l[:], ps[:, 6, :].rearrange("p (c n) -> p c n", c=KC),
                                      x3t_h[:].bitcast(F32), ALU.subtract).then_inc(x3t_lo, 1)

            pipelined(dve, iteration)

        @block.tensor
        def _(pe):
            def product(out_ap, a_h, a_l, b_h, b_l, start, stop):
                pe.matmul(out_ap, a_h, b_h, start=start, stop=False)
                pe.matmul(out_ap, a_h, b_l, start=False, stop=False)
                return pe.matmul(out_ap, a_l, b_h, start=False, stop=stop)

            pe.wait_ge(set_up, 2)
            pe.matmul(ps[:, 0, 0:NA], const("before"), onehot[:], start=True, stop=True)
            pe.matmul(ps[:, 0, NA:2 * NA], const("ones"), onehot[:], start=True, stop=True).then_inc(route_ps, 1)
            pe.wait_ge(set_up, MATCH_STEP)
            pe.matmul(ps[0:1, 2, 0:NSLOT], const("ones")[:, 0:1], match, start=True, stop=True)
            pe.matmul(ps[0:1, 1, 0:NSLOT], const("sample"), match, start=True, stop=True).then_inc(route_ps, 1)

            def adapter_product(i, u, again):
                a = pe.value_load(tile_adapter[0:1, bass.ds(i * XB + u, 1)], min_val=0, max_val=NA - 1)
                pe.wait_ge(w_ready, a + 1)
                pe.wait_ge(xt_ready, i * XB + u + 1)
                if again:
                    pe.wait_ge(y_copied, i * XB + (u - XB + 1))
                for c in range(KC):
                    last = pe.matmul(ps[:, 4 + u, :], xt_sb[u % 2][:, c].rearrange("p s t -> p (s t)"),
                                     w_all[:, bass.ds(a, 1), c, :], start=(c == 0), stop=(c == KC - 1))
                last.then_inc(y_ps, 1)

            pe.wait_ge(routed, 1)
            for u in range(XB):
                adapter_product(0, u, False)
            with pe.Fori(1, ST // XB) as i:
                for u in range(XB):
                    adapter_product(i, u, True)

            pe.wait_ge(wqkv_lo, 1)
            pe.wait_ge(y_copied, ST)
            pe.wait_ge(mix_in, 16 * NB)

            def y_transpose(t, p, k):
                if has(t):
                    pe.wait_ge(y_in[p], k * 16 + 16)
                    need(pe, cxt_lo, t - 2)
                    for c in range(KC):
                        last = pe.transpose(ps[:, 0, c * P:(c + 1) * P], y_nat[p][:, c * P:(c + 1) * P], ident)
                    last.then_inc(yt_ps, 1)

            y_transpose(0, 0, 0)

            def scores(t, half):
                pe.matmul(ps[:, 3 + half, :], ident_bf[:], causal_bf[:], start=True, stop=False)
                for s in range(2 * half, 2 * half + 2):
                    n = (s % 2) * KV * T
                    last = pe.matmul(ps[:, 3 + half, n:n + KV * T], qt[:, s, :], k_bd[:, s].rearrange("p h t -> p (h t)"),
                                     start=False, stop=(s % 2 == 1))
                if half:
                    last.then_inc(scores_ps, 1)

            def iteration(i, p, k):
                if has(i):
                    pe.wait_ge(yt_lo, i + 1)
                    need(pe, qt_ready, i)
                    need(pe, k_ready, i)
                    for c in range(KC):
                        a_h, a_l = yt_h[:, c, :], yt_l[:, c, :]
                        product(ps[:, 1, :], a_h, a_l, wqkv_h[:, c, 0:NQ], wqkv_l[:, c, 0:NQ], c == 0, c == KC - 1)
                        last = product(ps[:, 2, 0:2 * NKV], a_h, a_l, wqkv_h[:, c, NQ:NQKV], wqkv_l[:, c, NQ:NQKV],
                                       c == 0, c == KC - 1)
                    last.then_inc(qkv_ps, 1)
                if has(i - 2):
                    pe.wait_ge(x3t_lo, i - 1)
                    pe.wait_ge(x2_ready, i - 1)
                    for c in range(KC):
                        last = product(ps[:, 5, 0:ER + E], x3t_h[:, c, :], x3t_l[:, c, :], wf_h[:, c, D:NF], wf_l[:, c, D:NF],
                                       c == 0, c == KC - 1)
                    last.then_inc(h_ps, 1)
                if has(i - 1):
                    pe.wait_ge(exp_ready, i)
                    for h in range(KV):
                        n = (h % 4) * P
                        last = pe.transpose(ps[:, 3 + h // 4, n:n + P], prob[:, h].rearrange("p s t -> p (s t)"), ident)
                    last.then_inc(pt_ps, 1)
                y_transpose(i + 1, 1 - p, k + p if not isinstance(i, int) else (i + 1) // 2)
                if has(i - 2):
                    need(pe, out_ready, i - 2)
                    for c in range(KC):
                        product(ps[:, 7, :], x3t_h[:, c, :], x3t_l[:, c, :], wf_h[:, c, 0:D], wf_l[:, c, 0:D],
                                c == 0, False)
                if has(i - 1):
                    pe.wait_ge(pt_lower, i)
                    pe.wait_ge(pt_upper, i)
                    pe.wait_ge(v_ready, i)
                    for h in range(KV):
                        n = (h % 4) * P
                        last = pe.matmul(ps[:, 3 + h // 4, n:n + SPT * VW], pt[:, h, :],
                                         v_bd[1 - p][:, h].rearrange("p s w -> p (s w)"), start=True, stop=True)
                    last.then_inc(cx_ps, 1)
                if has(i - 2):
                    pe.wait_ge(hw_ready, i - 1)
                    pe.transpose(ps[:, 6, 0:P], hw[:].rearrange("p e r -> p (e r)"), ident).then_inc(hwt_ps, 1)
                if has(i - 1):
                    pe.wait_ge(cx_ready, i)
                    need(pe, yt_lo, min(i + 2, NT) if isinstance(i, int) else i + 2)
                    for s in range(SPT):
                        last = pe.transpose(ps[:, 0, s * P:(s + 1) * P], cx[:, s].rearrange("p h d -> p (h d)"), ident)
                    last.then_inc(cxt_ps, 1)
                if has(i - 2):
                    pe.wait_ge(hwt_ready, i - 1)
                    pe.matmul(ps[:, 7, :], hwt[:], wb_sb[:], start=False, stop=True).then_inc(out_ps, 1)
                if has(i):
                    pe.wait_ge(roped, i + 1)
                    pe.wait_ge(v_ready, i + 1)
                    for g in range(G):
                        pe.transpose(ps[:, 1, g * P:(g + 1) * P], qk[:, g * P:(g + 1) * P], ident)
                    pe.transpose(ps[:, 2, 0:P], qk[:, NQ:NQK], ident).then_inc(qkt_ps, 1)
                if isinstance(i, int) and i == 1:
                    pe.wait_ge(w2_lo, 1)
                if has(i - 1):
                    pe.wait_ge(cxt_lo, i)
                    need(pe, hw_ready, i - 1)
                    for g in range(G):
                        last = product(ps[:, 5, :], cxt_h[:, g].rearrange("p s t -> p (s t)"),
                                       cxt_l[:, g].rearrange("p s t -> p (s t)"), wo_h[:, g, :], wo_l[:, g, :],
                                       g == 0, g == G - 1)
                    last.then_inc(wo_ps, 1)
                if has(i):
                    pe.wait_ge(qt_ready, i + 1)
                    pe.wait_ge(k_ready, i + 1)
                    need(pe, cx_ready, i)
                    scores(i, 0)
                if has(i - 1):
                    pe.wait_ge(x2_ready, i)
                    need(pe, hwt_ready, i - 1)
                    mix = mix_bd[:, i - 1, :] if isinstance(i, int) else \
                        mix_bd[:, bass.ds(i - 1, 1), :].rearrange("p a n -> p (a n)")
                    for c in range(KC):
                        last = pe.matmul(ps[:, 6, c * P:(c + 1) * P], x2[:, c * P:(c + 1) * P], mix, start=True, stop=True)
                    last.then_inc(x3t_ps, 1)
                if has(i):
                    scores(i, 1)

            pipelined(pe, iteration)


MATCH_STEP = 13


def kernel(x, itok_B_1_14, itok_B_0_15, L0_cond_weight, L0_attn_Wq, L0_attn_Wk, L0_attn_Wv, L0_attn_Wo,
           L0_cond2_weights, L0_ffn_W_base, L0_ffn_b_base, L0_ffn_W_gate, L0_ffn_A, L0_ffn_B):
    import concourse.bacc as bacc
    from concourse.bass_utils import run_bass_kernel_spmd

    def chunked(w):
        return w.reshape(KC, P, w.shape[1]).transpose(1, 0, 2)

    a = np.asarray
    x = a(x)
    consts, where = constants()
    wq = a(L0_attn_Wq).reshape(D, KV, G, HD).transpose(0, 2, 1, 3).reshape(D, NQ)
    arrays = {
        "x": x.reshape(NB * T, D),
        "xt": x.reshape(NB, T, KC, P).transpose(0, 3, 2, 1).reshape(NB * P, KC * T),
        "ids_a": a(itok_B_1_14),
        "ids_m": a(itok_B_0_15),
        "wcond": a(L0_cond_weight).transpose(0, 2, 1).reshape(NA, KC, P, D).transpose(0, 2, 1, 3),
        "wqkv": chunked(np.concatenate([wq, a(L0_attn_Wk), a(L0_attn_Wv)], 1)),
        "wo": a(L0_attn_Wo).reshape(KV, G, HD, D).transpose(0, 2, 1, 3).reshape(P, G, D),
        "wmix": a(L0_cond2_weights).reshape(NA * T, T),
        "wffn": chunked(np.concatenate([a(L0_ffn_W_base).T, a(L0_ffn_A).reshape(ER, D).T, a(L0_ffn_W_gate).T], 1)),
        "wb": a(L0_ffn_B).transpose(0, 2, 1).reshape(ER, D),
        "bias": a(L0_ffn_b_base),
        "consts": consts,
    }
    arrays = {name: np.ascontiguousarray(v) for name, v in arrays.items()}
    nc = bacc.Bacc("TRN2", target_bir_lowering=False, num_devices=1)
    args = [nc.dram_tensor(name, v.shape, mybir.dt.from_np(v.dtype), kind="ExternalInput").ap()
            for name, v in arrays.items()]
    out = nc.dram_tensor("out", (NB * T, D), F32, kind="ExternalOutput").ap()
    build(nc, *args, out, where)
    result = run_bass_kernel_spmd(nc, [arrays], core_ids=[0])
    return result.results[0]["out"].reshape(NB, T, D)
```

```python
from contextlib import ExitStack

import numpy as np

import concourse.bass as bass
from concourse import mybir

F32 = mybir.dt.float32
F32R = mybir.dt.float32r
BF16 = mybir.dt.bfloat16
I32 = mybir.dt.int32
U32 = mybir.dt.uint32
ALU = mybir.AluOpType
ACT = mybir.ActivationFunctionType
X = mybir.AxisListType.X

P = 128
NB, T, D = 128, 32, 512
KC = D // P
NA = 16
SPT = P // T
NT = NB // SPT
ST = (NB + NA * (SPT - 1)) // SPT
NSLOT = ST * SPT
KV, G, HD = 8, 4, 16
HALF = HD // 2
NQ, NKV = KV * G * HD, KV * HD
NQK = NQ + NKV
NQKV = NQ + 2 * NKV
E, R = 8, 16
ER = E * R
NF = D + ER + E
NFH = NF // 2
VW = HD + 1
XB = 4
NEG = -1.0e30
ROPE_BASE = 500000.0


def constants():
    p = np.arange(P)
    slot = np.arange(NSLOT)
    inv = (1.0 / ROPE_BASE ** (np.arange(0, HD, 2, dtype=np.float32) / HD)).astype(np.float32)
    angle = ((p % T).astype(np.float32)[:, None] * inv[None, :]).astype(np.float32)
    cos, sin = np.cos(angle), np.sin(angle)
    rows = np.ones((P, 1))
    a = np.arange(NA)
    parts = {
        "ident": np.eye(P),
        "cos": np.concatenate([cos, cos], 1),
        "sin": np.concatenate([-sin, sin], 1),
        "kvmask": (p[:, None] // HD == np.arange(KV)[None, :]),
        "own_sample": (p[:, None] // T == np.arange(SPT)[None, :]),
        "before": (p[:, None] < p[None, :]),
        "ones": np.ones((P, P)),
        "causal": np.where(np.arange(T)[None, :] > (p % T)[:, None], NEG, 0.0),
        "iota_a": rows * a,
        "rev_e": rows * (E - np.arange(E)),
        "four_m": rows * (SPT * np.arange(NB // SPT)),
        "upto": rows * (a[None, :] <= a[:, None]).reshape(1, -1),
        "iota_slot": rows * slot,
        "iota_tile": rows * np.arange(ST),
        "sample": p[:, None],
        "sample_row": np.repeat(p[:, None] * T, T, 1),
        "pad_row": (NB + SPT * np.arange(ST)[None, :] + p[:, None] // T) * T,
        "token": p[:, None] % T,
    }
    at, where = 0, {}
    for name, v in parts.items():
        where[name] = (at, v.shape[1])
        at += v.shape[1]
    return np.ascontiguousarray(np.concatenate([np.asarray(v, np.float32) for v in parts.values()], 1)), where


def build(nc, x, xt, ids_a, ids_m, wcond, wqkv, wo, wmix, wffn, wb, bias, consts, out, where):
    ncols = consts.shape[1]
    with ExitStack() as ctx:
        def sb(name, shape, dt=F32):
            return ctx.enter_context(nc.sbuf_tensor(name, shape, dt))

        def sem(name):
            return ctx.enter_context(nc.semaphore(name))

        ps = ctx.enter_context(nc.psum_tensor("ps", [P, 8, 512], F32))
        y_rows = nc.dram_tensor("y_rows", ((NB + NSLOT) * T, D), F32, kind="Internal").ap()

        cst = sb("cst", [P, ncols])

        def const(name):
            a, n = where[name]
            return cst[:, a:a + n]

        ident = const("ident")
        ident_bf = sb("ident_bf", [P, P], BF16)
        causal_bf = sb("causal_bf", [P, T], BF16)
        wqkv_h = sb("wqkv_h", [P, KC, NQKV], F32R)
        wqkv_l = sb("wqkv_l", [P, KC, NQKV], F32R)
        mix_bd = sb("mix_bd", [P, NT, P])

        stage1 = ExitStack()
        def sb1(name, shape, dt=F32):
            return stage1.enter_context(nc.sbuf_tensor(name, shape, dt))
        w_all = sb1("w_all", [P, NA, KC, D])
        xt_raw = [sb1(f"xt_raw{u}", [P, SPT, KC, T]) for u in range(XB)]
        xt_sb = [sb1(f"xt_sb{p}", [P, KC, SPT, T]) for p in range(2)]
        y_sb = [sb1(f"y_sb{u}", [P, D]) for u in range(2)]
        wqkv_raw = sb1("wqkv_raw", [P, KC, NQKV])
        wide = w_all[:, NA - 1].rearrange("p c n -> p (c n)")[:, 0:ST * NA]
        mix_own = wqkv_raw[:].rearrange("p c n -> p (c n)")[:, 0:NT * T].rearrange("p (g d) -> p g d", d=T)
        mix_sum = wqkv_raw[:].rearrange("p c n -> p (c n)")[:, NT * T:2 * NT * T].rearrange("p (g d) -> p g d", d=T)
        wmix_sb = sb1("wmix_sb", [P, NA, T])
        ids_mix = sb1("ids_mix", [P, NT])
        idsm_f = sb1("idsm_f", [1, NB])
        ids_col = sb1("ids_col", [P, 1], I32)
        idsm_row = sb1("idsm_row", [1, NB], I32)
        idsf = sb1("idsf", [P, 1])
        onehot = sb1("onehot", [P, NA])
        tiles_a = sb1("tiles_a", [P, NA])
        end_a = sb1("end_a", [P, NA])
        base_a = sb1("base_a", [P, NA])
        pos_a = sb1("pos_a", [P, NA])
        pos = sb1("pos", [P, 1])
        match = wide[:, 0:NSLOT]
        adapter_f = sb1("adapter_f", [P, ST])
        tile_adapter = sb1("tile_adapter", [P, ST], I32)
        slot_sample = sb1("slot_sample", [1, NSLOT], I32)
        pad = wide[:, NSLOT:NSLOT + ST]
        y_row = sb1("y_row", [P, ST], U32)
        stage1.close()

        y_nat = [sb(f"y_nat{p}", [P, D]) for p in range(2)]
        x_nat = [sb(f"x_nat{p}", [P, D]) for p in range(2)]
        yt_h = sb("yt_h", [P, KC, P], F32R)
        yt_l = sb("yt_l", [P, KC, P], F32R)
        rope_a = sb("rope_a", [P, NQK])
        rope_b = sb("rope_b", [P, NQK])
        qk = sb("qk", [P, NQK])
        v_bd = [sb(f"v_bd{p}", [P, KV, SPT, VW]) for p in range(2)]
        qt = sb("qt", [P, SPT, P])
        k_bd = sb("k_bd", [P, SPT, KV, T])
        row_max = sb("row_max", [P, SPT * KV])
        prob = sb("prob", [P, KV, SPT, T])
        pt = sb("pt", [P, KV, P])
        recip = sb("recip", [P, KV, SPT])
        cx = sb("cx", [P, SPT, KV, HD])
        cxt_h = sb("cxt_h", [P, G, SPT, T], F32R)
        cxt_l = sb("cxt_l", [P, G, SPT, T], F32R)
        x2 = sb("x2", [P, D])
        x2b = [sb(f"x2b{p}", [P, D]) for p in range(2)]
        x3t_h = sb("x3t_h", [P, KC, P], F32R)
        x3t_l = sb("x3t_l", [P, KC, P], F32R)
        logit = sb("logit", [P, E])
        logit2 = sb("logit2", [P, E])
        first = sb("first", [P, E])
        second = sb("second", [P, E])
        pick = sb("pick", [P, E])
        route = sb("route", [P, E])
        rs = sb("rs", [P, 8])
        hw = sb("hw", [P, E, R])
        hwt = sb("hwt", [P, P])
        o_sb = [sb(f"o_sb{p}", [P, D]) for p in range(2)]
        wo_raw = sb("wo_raw", [P, G, D])
        wo_h = sb("wo_h", [P, G, D], F32R)
        wo_l = sb("wo_l", [P, G, D], F32R)
        wf_raw = sb("wf_raw", [P, KC, NF])
        wf_h = sb("wf_h", [P, KC, NF], F32R)
        wf_l = sb("wf_l", [P, KC, NF], F32R)
        wb_sb = sb("wb_sb", [P, D])
        bias_sb = sb("bias_sb", [P, D])

        cst_in = sem("cst_in")
        ids_in = sem("ids_in")
        w_in = [sem(f"w_in{a}") for a in range(NA)]
        wqkv_in = sem("wqkv_in")
        xt_in = [sem(f"xt_in{u}") for u in range(XB)]
        wmix_in = sem("wmix_in")
        mix_part = sem("mix_part")
        mix_added = sem("mix_added")
        mix_ready = sem("mix_ready")
        w2_in = sem("w2_in")
        y_in = [sem(f"y_in{p}") for p in range(2)]
        x_in = [sem(f"x_in{p}") for p in range(2)]
        set_up = sem("set_up")
        route_ps = sem("route_ps")
        routed = sem("routed")
        w_ready = sem("w_ready")
        xt_ready = sem("xt_ready")
        y_ps = sem("y_ps")
        y_copied = sem("y_copied")
        y_stored = [sem(f"y_stored{u}") for u in range(2)]
        zeroed = sem("zeroed")
        wqkv_hi = sem("wqkv_hi")
        wqkv_lo = sem("wqkv_lo")
        w2_hi = sem("w2_hi")
        w2_lo = sem("w2_lo")
        yt_ps, yt_hi, yt_lo = sem("yt_ps"), sem("yt_hi"), sem("yt_lo")
        qkv_ps, roped_parts, roped, v_ready = sem("qkv_ps"), sem("roped_parts"), sem("roped"), sem("v_ready")
        qkt_ps, qt_ready, k_ready = sem("qkt_ps"), sem("qt_ready"), sem("k_ready")
        scores_ps, max_ready, shifted, exp_ready = sem("scores_ps"), sem("max_ready"), sem("shifted"), sem("exp_ready")
        pt_ps, pt_lower, pt_upper = sem("pt_ps"), sem("pt_lower"), sem("pt_upper")
        cx_ps, recip_ready, cx_ready = sem("cx_ps"), sem("recip_ready"), sem("cx_ready")
        cxt_ps, cxt_hi, cxt_lo = sem("cxt_ps"), sem("cxt_hi"), sem("cxt_lo")
        wo_ps, x2_ready, x2b_ready = sem("wo_ps"), sem("x2_ready"), sem("x2b_ready")
        x3t_ps, x3t_hi, x3t_lo = sem("x3t_ps"), sem("x3t_hi"), sem("x3t_lo")
        h_ps, route_step, gate_exp = sem("h_ps"), sem("route_step"), sem("gate_exp")
        hw_ready, hwt_ps, hwt_ready = sem("hw_ready"), sem("hwt_ps"), sem("hwt_ready")
        out_ps, out_ready = sem("out_ps"), sem("out_ready")
        out_stored = [sem(f"out_stored{p}") for p in range(2)]

        RSTEPS = 12

        def need(eng, s, n):
            if not isinstance(n, int) or n > 0:
                eng.wait_ge(s, n)

        def numbers(engine, ap, top):
            return nc.values_load_multi_w_load_instructions(ap, engines=[engine], min_val=0, max_val=top)[1]

        def has(t):
            return not isinstance(t, int) or 0 <= t < NT

        def pipelined(eng, iteration, ahead=1):
            for i in range(4):
                iteration(i, i % 2, i // 2)
            with eng.Fori(2, NT // 2 - ahead) as k:
                for u in range(2):
                    iteration(k * 2 + u, u, k)
            for i in range(NT - 2 * ahead, NT + 3):
                iteration(i, i % 2, i // 2)

        block = ctx.enter_context(nc.Block())

        @block.sync
        def _(sp):
            sp.dma_start(ids_col[:], ids_a.rearrange("(p a) -> p a", a=1)).then_inc(ids_in, 16)
            sp.dma_start(idsm_row[:], ids_m.rearrange("(a p) -> a p", a=1)).then_inc(ids_in, 16)
            sp.dma_start(cst[:], consts).then_inc(cst_in, 16)
            for j in range(SPT):
                sp.dma_start(wmix_sb[j * T:(j + 1) * T], wmix.rearrange("(a c) d -> c a d", a=NA)).then_inc(wmix_in, 16)
            sp.wait_ge(routed, 1)

            def gather(i, u, again):
                regs = numbers(mybir.EngineType.SP, slot_sample[0:1, bass.ds((i * XB + u) * SPT, SPT)], NB - 1)
                for j in range(SPT):
                    if again and j == 0:
                        sp.wait_ge(xt_ready, i * XB + (u - XB + 1))
                    sp.dma_start(xt_raw[u][:, j].rearrange("p c t -> p (c t)"), xt[bass.ds(regs[j] * P, P), :]).then_inc(xt_in[u], 16)

            for u in range(XB):
                gather(0, u, False)
            with sp.Fori(1, ST // XB) as i:
                for u in range(XB):
                    gather(i, u, True)

            sp.wait_ge(y_ps, ST)
            sp.wait_ge(y_copied, ST)
            sp.wait_ge(mix_ready, SPT)
            sp.wait_ge(wqkv_lo, 1)
            for u in range(2):
                sp.wait_ge(y_stored[u], 16 * (ST // 2))

            def rows(t):
                return bass.ds(t * P, P)

            def load_y(t, p):
                if has(t):
                    need(sp, yt_ps, t - 1)
                    sp.dma_start(y_nat[p][:], y_rows[rows(t), :]).then_inc(y_in[p], 16)

            def load_x(t, p):
                if has(t):
                    need(sp, x2_ready, t - 1)
                    sp.dma_start(x_nat[p][:], x[rows(t), :]).then_inc(x_in[p], 16)

            load_y(0, 0)
            load_y(1, 1)
            load_x(0, 0)
            sp.dma_start(wo_raw[:], wo).then_inc(w2_in, 16)
            sp.dma_start(wf_raw[:], wffn).then_inc(w2_in, 16)
            sp.dma_start(wb_sb[:], wb).then_inc(w2_in, 16)
            sp.dma_start(bias_sb[:], bias.rearrange("(a d) -> a d", a=1).broadcast_to([P, D])).then_inc(w2_in, 16)
            load_y(2, 0)

            def iteration(i, p, k):
                load_y(i + 3, 1 - p)
                if has(i - 3):
                    sp.wait_ge(out_ready, i - 2)
                    sp.dma_start(out[rows(i - 3), :], o_sb[1 - p][:]).then_inc(out_stored[1 - p], 16)
                load_x(i + 1, 1 - p)

            pipelined(sp, iteration, ahead=2)
            for p in range(2):
                sp.wait_ge(out_stored[p], 16 * (NT // 2))

        @block.gpsimd
        def _(pool):
            pool.memset(mix_bd[:], 0.0).then_inc(zeroed, 1)

            def store_y(t):
                pool.wait_ge(y_copied, t + 1)
                pool.indirect_dma_start(y_rows[:, :], bass.IndirectOffsetOnAxis(ap=y_row[:, t:t + 1], axis=0),
                                        y_sb[t % 2][:], None).then_inc(y_stored[t % 2], 16)

            pool.wait_ge(routed, 2)
            for t in range(ST):
                store_y(t)
                if t == MIX_FROM:
                    pool.wait_ge(wqkv_lo, 1)
                    pool.memset(mix_sum, 0.0).then_inc(mix_added, 1)
                if t > MIX_FROM and (t - MIX_FROM) % 2 == 0 and (t - MIX_FROM) // 2 <= NA:
                    n = (t - MIX_FROM) // 2
                    pool.wait_ge(mix_part, n)
                    pool.wait_ge(mix_added, n)
                    pool.tensor_tensor(mix_sum, mix_sum, mix_own, ALU.add).then_inc(mix_added, 1)

            pool.wait_ge(y_ps, ST)
            for u in range(2):
                pool.wait_ge(y_stored[u], 16 * (ST // 2))
            pool.wait_ge(mix_ready, SPT)
            pool.wait_ge(wqkv_lo, 1)
            for p in range(2):
                pool.memset(v_bd[p][:], 0.0).then_inc(zeroed, 1)
            pool.wait_ge(zeroed, 3)
            for p in range(2):
                pool.tensor_copy(v_bd[p][:, :, :, HD], const("own_sample").rearrange("p (h s) -> p h s", h=1)
                                 .broadcast_to([P, KV, SPT])).then_inc(zeroed, 1)

            def iteration(i, p, k):
                if has(i):
                    pool.wait_ge(roped_parts, i + 1)
                    need(pool, qkt_ps, i)
                    pool.tensor_tensor(qk[:], rope_a[:], rope_b[:], ALU.add).then_inc(roped, 1)
                if has(i - 1):
                    if isinstance(i, int) and i == 1:
                        pool.wait_ge(w2_in, 64)
                    pool.wait_ge(x2_ready, i)
                    need(pool, out_ready, i - 2)
                    pool.tensor_tensor(x2b[1 - p][:], x2[:], bias_sb[:], ALU.add).then_inc(x2b_ready, 1)

            pipelined(pool, iteration)

        @block.scalar
        def _(act):
            act.wait_ge(cst_in, 16)
            for a in range(3):
                act.dma_start(w_all[:, a], wcond[a]).then_inc(w_in[a], 16)
            act.dma_start(wqkv_raw[:], wqkv).then_inc(wqkv_in, 16)
            for a in range(NA):
                act.wait_ge(w_in[a], 16)
                act.sem_inc(w_ready, 1)
                if a + 3 == NA - 1:
                    act.wait_ge(route_ps, 4)
                    act.wait_ge(routed, 2)
                if a + 3 < NA:
                    act.dma_start(w_all[:, a + 3], wcond[a + 3]).then_inc(w_in[a + 3], 16)
                if a == 3:
                    act.wait_ge(wqkv_in, 16)
                    act.activation(wqkv_h[:], wqkv_raw[:], ACT.Copy).then_inc(wqkv_hi, 1)

            act.wait_ge(zeroed, 1)
            act.wait_ge(mix_added, NA + 1)
            for j in range(SPT):
                q = slice(j * T, (j + 1) * T)
                act.activation(mix_bd[q, :, q], mix_sum[q], ACT.Copy).then_inc(mix_ready, 1)

            act.wait_ge(y_ps, ST)
            for u in range(2):
                act.wait_ge(y_stored[u], 16 * (ST // 2))
            act.wait_ge(mix_ready, SPT)
            act.wait_ge(wqkv_lo, 1)

            def split_hi(t):
                if has(t):
                    act.wait_ge(yt_ps, t + 1)
                    need(act, qkv_ps, t)
                    act.activation(yt_h[:], ps[:, 0, :].rearrange("p (c n) -> p c n", c=KC), ACT.Copy).then_inc(yt_hi, 1)

            split_hi(0)

            def iteration(i, p, k):
                if has(i - 1):
                    act.wait_ge(shifted, i)
                    act.activation(prob[:], prob[:], ACT.Exp, scale=HD ** -0.5).then_inc(exp_ready, 1)
                if has(i - 3):
                    act.wait_ge(hwt_ps, i - 2)
                    need(act, out_ps, i - 3)
                    act.activation(hwt[:], ps[:, 6, 0:P], ACT.Copy).then_inc(hwt_ready, 1)
                split_hi(i + 1)
                if has(i - 1):
                    act.wait_ge(pt_ps, i)
                    need(act, cx_ps, i - 1)
                    act.activation(pt[:, 0:KV // 2], ps[:, 3, :].rearrange("p (h n) -> p h n", h=KV // 2),
                                   ACT.Copy).then_inc(pt_lower, 1)
                if has(i):
                    act.wait_ge(roped_parts, i + 1)
                    if isinstance(i, int) and i == 0:
                        act.wait_ge(zeroed, 5)
                    need(act, cx_ps, i - 1)
                    for j in range(SPT):
                        q = slice(j * T, (j + 1) * T)
                        last = act.activation(v_bd[p][q, :, j, 0:HD],
                                              ps[q, 2, NKV:2 * NKV].rearrange("p (h d) -> p h d", h=KV), ACT.Copy)
                    last.then_inc(v_ready, 1)
                    act.wait_ge(qkt_ps, i + 1)
                    need(act, scores_ps, i)
                    act.activation(qt[:].rearrange("p s (g t) -> p s g t", g=G),
                                   ps[:, 1, :].rearrange("p (g s t) -> p s g t", s=SPT, g=G), ACT.Copy).then_inc(qt_ready, 1)
                if has(i - 1):
                    act.wait_ge(cxt_ps, i)
                    need(act, wo_ps, i - 1)
                    act.activation(cxt_h[:].rearrange("p g s t -> p s g t"),
                                   ps[:, 0, :].rearrange("p (s g t) -> p s g t", s=SPT, g=G), ACT.Copy).then_inc(cxt_hi, 1)
                if has(i - 2):
                    act.wait_ge(route_step, (i - 2) * RSTEPS + 7)
                    act.activation(rs[:, 4:5], rs[:, 0:1], ACT.Exp, bias=rs[:, 2:3], scale=-1.0).then_inc(gate_exp, 1)
                if isinstance(i, int) and i == 0:
                    act.wait_ge(w2_in, 64)
                    act.activation(wo_h[:], wo_raw[:], ACT.Copy)
                    act.activation(wf_h[:], wf_raw[:], ACT.Copy).then_inc(w2_hi, 1)
                if has(i - 1):
                    act.wait_ge(x3t_ps, i)
                    need(act, h_ps, i - 1)
                    act.activation(x3t_h[:], ps[:, 6, :].rearrange("p (c n) -> p c n", c=KC), ACT.Copy).then_inc(x3t_hi, 1)

            pipelined(act, iteration)

        @block.vector
        def _(dve):
            steps = [0]

            def then(ins):
                steps[0] += 1
                ins.then_inc(set_up, 1)
                dve.wait_ge(set_up, steps[0])

            dve.wait_ge(ids_in, 32)
            dve.tensor_copy(idsm_f[:], idsm_row[:])
            then(dve.tensor_copy(idsf[:], ids_col[:]))
            dve.wait_ge(cst_in, 16)
            then(dve.tensor_scalar(onehot[:], const("iota_a"), idsf[:, 0:1], None, ALU.is_equal))
            dve.tensor_copy(ident_bf[:], ident)
            dve.tensor_copy(causal_bf[:], const("causal"))
            dve.wait_ge(route_ps, 1)
            wide_m = wide[:, 0:NA * NT].rearrange("p (a m) -> p a m", a=NA)
            count = ps[:, 0, NA:2 * NA].rearrange("p (a m) -> p a m", m=1).broadcast_to([P, NA, NT])
            four = const("four_m").rearrange("p (a m) -> p a m", a=1).broadcast_to([P, NA, NT])
            then(dve.tensor_tensor(wide_m, count, four, ALU.is_gt))
            then(dve.tensor_reduce(tiles_a[:], wide_m, X, ALU.add))
            wide_a = wide[:, 0:NA * NA].rearrange("p (a b) -> p a b", a=NA)
            upto = const("upto").rearrange("p (a b) -> p a b", a=NA)
            then(dve.tensor_tensor(wide_a, upto, tiles_a[:].rearrange("p (a b) -> p a b", a=1).broadcast_to([P, NA, NA]),
                                   ALU.mult))
            then(dve.tensor_reduce(end_a[:], wide_a, X, ALU.add))
            then(dve.tensor_tensor(base_a[:], end_a[:], tiles_a[:], ALU.subtract))
            then(dve.scalar_tensor_tensor(pos_a[:], base_a[:], float(SPT), ps[:, 0, 0:NA], ALU.mult, ALU.add))
            then(dve.tensor_tensor(pos_a[:], pos_a[:], onehot[:], ALU.mult))
            then(dve.tensor_reduce(pos[:], pos_a[:], X, ALU.add))
            wide_t = wide[:, 0:ST * NA].rearrange("p (t a) -> p t a", a=NA)
            tile_no = const("iota_tile").rearrange("p (t a) -> p t a", a=1).broadcast_to([P, ST, NA])
            then(dve.tensor_tensor(wide_t, tile_no, end_a[:].rearrange("p (t a) -> p t a", t=1).broadcast_to([P, ST, NA]),
                                   ALU.is_ge))
            then(dve.tensor_reduce(adapter_f[:], wide_t, X, ALU.add))
            dve.tensor_scalar(tile_adapter[:], adapter_f[:], float(NA - 1), None, ALU.min)
            then(dve.tensor_scalar(match, const("iota_slot"), pos[:, 0:1], None, ALU.is_equal))
            assert steps[0] == MATCH_STEP
            dve.wait_ge(route_ps, 2)
            dve.tensor_copy(slot_sample[:], ps[0:1, 1, 0:NSLOT]).then_inc(routed, 1)
            dve.wait_ge(route_ps, 3)
            then(dve.tensor_scalar(pad, ps[:, 2, ST:2 * ST], -1.0, 1.0, ALU.mult, ALU.add))
            then(dve.tensor_tensor(pad, pad, const("pad_row"), ALU.mult))
            then(dve.tensor_tensor(pad, ps[:, 2, 0:ST], pad, ALU.add))
            dve.tensor_scalar(y_row[:], pad, const("token"), None, ALU.add).then_inc(routed, 1)
            dve.wait_ge(route_ps, 4)
            then(dve.tensor_copy(ids_mix[:], ps[:, 3, 0:NT]))

            def order_x(i, u, again):
                dve.wait_ge(xt_in[u], i * 64 + 64)
                if again or u >= 2:
                    dve.wait_ge(y_ps, i * XB + (u - 1))
                dve.tensor_copy(xt_sb[u % 2][:].rearrange("p c s t -> p s c t"), xt_raw[u][:]).then_inc(xt_ready, 1)

            def copy_y(i, u, again):
                dve.wait_ge(y_ps, i * XB + u + 1)
                if again or u >= 2:
                    dve.wait_ge(y_stored[u % 2], i * 32 + 16 * (u // 2))
                dve.tensor_copy(y_sb[u % 2][:], ps[:, 4 + u, :]).then_inc(y_copied, 1)

            def mix_share(a, first=False):
                if not first:
                    dve.wait_ge(mix_added, a + 1)
                dve.scalar_tensor_tensor(
                    mix_own, ids_mix[:].rearrange("p (g d) -> p g d", d=1).broadcast_to([P, NT, T]),
                    const("iota_a")[:, bass.ds(a, 1)],
                    wmix_sb[:, bass.ds(a, 1), :].broadcast_to([P, NT, T]), ALU.is_equal, ALU.mult).then_inc(mix_part, 1)

            order_x(0, 0, False)
            for u in range(XB):
                if u + 1 < XB:
                    order_x(0, u + 1, False)
                else:
                    order_x(1, 0, True)
                copy_y(0, u, False)
            dve.wait_ge(wqkv_hi, 1)
            dve.tensor_tensor(wqkv_l[:], wqkv_raw[:], wqkv_h[:].bitcast(F32), ALU.subtract).then_inc(wqkv_lo, 1)
            dve.wait_ge(wmix_in, 16 * SPT)
            dve.wait_ge(wqkv_lo, 1)

            def slot_tiles(i, with_mix):
                for u in range(XB):
                    order_x(i if u + 1 < XB else i + 1, (u + 1) % XB, True)
                    copy_y(i, u, True)
                    if with_mix and u % 2 == 0:
                        mix_share(i * 2 + (u // 2 - 2))

            with dve.Fori(1, 1 + NA // 2) as i:
                slot_tiles(i, True)
            for i in range(1 + NA // 2, ST // XB - 1):
                slot_tiles(i, False)
            for u in range(XB):
                if u + 1 < XB:
                    order_x(ST // XB - 1, u + 1, True)
                copy_y(ST // XB - 1, u, True)

            for u in range(2):
                dve.wait_ge(y_stored[u], 16 * (ST // 2))
            dve.wait_ge(mix_ready, SPT)
            dve.wait_ge(wqkv_lo, 1)

            def split_lo(t):
                if has(t):
                    dve.wait_ge(yt_hi, t + 1)
                    dve.tensor_tensor(yt_l[:], ps[:, 0, :].rearrange("p (c n) -> p c n", c=KC),
                                      yt_h[:].bitcast(F32), ALU.subtract).then_inc(yt_lo, 1)

            split_lo(0)
            cos = const("cos").rearrange("p (h d) -> p h d", h=1).broadcast_to([P, NQK // HD, HD])
            sin = [const("sin")[:, s * HALF:(s + 1) * HALF].rearrange("p (h d) -> p h d", h=1)
                   .broadcast_to([P, NQK // HD, HALF]) for s in range(2)]
            banks12 = ps[:, 1:3, :].rearrange("p a n -> p (a n)")
            qk_ps = banks12[:, 0:NQK].rearrange("p (h d) -> p h d", d=HD)
            sc = ps[:, 3:5, :].rearrange("p a n -> p (a n)").rearrange("p (h t) -> p h t", t=T)
            cxp = ps[:, 3:5, :].rearrange("p a n -> p (a n)").rearrange("p (h w) -> p h w", h=KV)[:, :, 0:SPT * VW] \
                .rearrange("p h (s w) -> p h s w", s=SPT)
            rev = const("rev_e")

            def routing(t):
                at = [0]

                def step(ins):
                    at[0] += 1
                    ins.then_inc(route_step, 1)
                    dve.wait_ge(route_step, t * RSTEPS + at[0])

                max1, key1, max2, key2, e2, den, r1, r2 = (rs[:, n:n + 1] for n in range(8))
                dve.wait_ge(h_ps, t + 1)
                step(dve.tensor_copy(logit[:], ps[:, 5, NFH - E:NFH]))
                step(dve.tensor_reduce(max1, logit[:], X, ALU.max))
                step(dve.scalar_tensor_tensor(pick[:], logit[:], max1, rev, ALU.is_equal, ALU.mult))
                step(dve.tensor_reduce(key1, pick[:], X, ALU.max))
                step(dve.tensor_scalar(first[:], rev, key1, None, ALU.is_equal))
                step(dve.scalar_tensor_tensor(logit2[:], first[:], 3.0 * NEG, logit[:], ALU.mult, ALU.add))
                step(dve.tensor_reduce(max2, logit2[:], X, ALU.max))
                step(dve.scalar_tensor_tensor(pick[:], logit2[:], max2, rev, ALU.is_equal, ALU.mult))
                dve.tensor_reduce(key2, pick[:], X, ALU.max)
                dve.wait_ge(gate_exp, t + 1)
                step(dve.tensor_scalar(den, e2, 1.0, None, ALU.add))
                dve.tensor_scalar(second[:], rev, key2, None, ALU.is_equal)
                step(dve.reciprocal(r1, den))
                dve.tensor_scalar(route[:], first[:], r1, None, ALU.mult)
                step(dve.tensor_tensor(r2, e2, r1, ALU.mult))
                step(dve.scalar_tensor_tensor(route[:], second[:], r2, route[:], ALU.mult, ALU.add))
                assert at[0] == RSTEPS
                need(dve, hwt_ps, t)
                dve.tensor_tensor(hw[:], ps[:, 5, D - NFH:NFH - E].rearrange("p (e r) -> p e r", e=E),
                                  route[:].rearrange("p (e r) -> p e r", r=1).broadcast_to([P, E, R]),
                                  ALU.mult).then_inc(hw_ready, 1)

            def iteration(i, p, k):
                if has(i - 1):
                    dve.wait_ge(scores_ps, i)
                    dve.tensor_reduce(row_max[:], sc, X, ALU.max).then_inc(max_ready, 1)
                    dve.wait_ge(max_ready, i)
                    need(dve, pt_ps, i - 1)
                    dve.tensor_tensor(prob[:].rearrange("p h s t -> p s h t"), sc.rearrange("p (s h) t -> p s h t", h=KV),
                                      row_max[:].rearrange("p (s h t) -> p s h t", h=KV, t=1)
                                      .broadcast_to([P, SPT, KV, T]), ALU.subtract).then_inc(shifted, 1)
                if has(i):
                    dve.wait_ge(qkv_ps, i + 1)
                    need(dve, roped, i)
                    dve.tensor_tensor(rope_a[:].rearrange("p (h d) -> p h d", d=HD), qk_ps, cos, ALU.mult)
                    for s in range(2):
                        last = dve.tensor_tensor(
                            rope_b[:].rearrange("p (h d) -> p h d", d=HD)[:, :, s * HALF:(s + 1) * HALF],
                            qk_ps[:, :, (1 - s) * HALF:(2 - s) * HALF], sin[s], ALU.mult)
                    last.then_inc(roped_parts, 1)
                split_lo(i + 1)
                if has(i - 1):
                    dve.wait_ge(pt_ps, i)
                    need(dve, cx_ps, i - 1)
                    dve.tensor_copy(pt[:, KV // 2:KV], ps[:, 4, :].rearrange("p (h n) -> p h n", h=KV // 2)) \
                       .then_inc(pt_upper, 1)
                if has(i - 3):
                    dve.wait_ge(out_ps, i - 2)
                    dve.wait_ge(x2b_ready, i - 2)
                    need(dve, out_stored[1 - p], k * 16 + 16 * p - 32)
                    dve.tensor_tensor(o_sb[1 - p][:, 0:NFH], ps[:, 7, 0:NFH], x2b[1 - p][:, 0:NFH], ALU.add)
                    dve.tensor_tensor(o_sb[1 - p][:, NFH:D], ps[:, 5, 0:D - NFH], x2b[1 - p][:, NFH:D], ALU.add) \
                       .then_inc(out_ready, 1)
                if has(i - 1):
                    dve.wait_ge(cx_ps, i)
                    dve.reciprocal(recip[:], cxp[:, :, :, HD]).then_inc(recip_ready, 1)
                    dve.wait_ge(recip_ready, i)
                    need(dve, cxt_ps, i - 1)
                    dve.tensor_tensor(cx[:].rearrange("p s h d -> p h s d"), cxp[:, :, :, 0:HD],
                                      recip[:].rearrange("p h (s d) -> p h s d", d=1).broadcast_to([P, KV, SPT, HD]),
                                      ALU.mult).then_inc(cx_ready, 1)
                if has(i):
                    dve.wait_ge(qkt_ps, i + 1)
                    need(dve, scores_ps, i)
                    kt = ps[:, 2, 0:P].rearrange("p (s h t) -> p s h t", s=SPT, h=1).broadcast_to([P, SPT, KV, T])
                    mask = const("kvmask").rearrange("p (s h t) -> p s h t", s=1, t=1).broadcast_to([P, SPT, KV, T])
                    dve.tensor_tensor(k_bd[:], kt, mask, ALU.mult).then_inc(k_ready, 1)
                if has(i - 1):
                    dve.wait_ge(cxt_hi, i)
                    dve.tensor_tensor(cxt_l[:].rearrange("p g s t -> p s g t"),
                                      ps[:, 0, :].rearrange("p (s g t) -> p s g t", s=SPT, g=G),
                                      cxt_h[:].bitcast(F32).rearrange("p g s t -> p s g t"), ALU.subtract).then_inc(cxt_lo, 1)
                if has(i - 2):
                    routing(i - 2)
                if isinstance(i, int) and i == 0:
                    dve.wait_ge(w2_hi, 1)
                    dve.tensor_tensor(wo_l[:], wo_raw[:], wo_h[:].bitcast(F32), ALU.subtract)
                    dve.tensor_tensor(wf_l[:], wf_raw[:], wf_h[:].bitcast(F32), ALU.subtract).then_inc(w2_lo, 1)
                if has(i - 1):
                    dve.wait_ge(wo_ps, i)
                    dve.wait_ge(x_in[1 - p], k * 16 + 16 * p)
                    need(dve, x3t_ps, i - 1)
                    need(dve, x2b_ready, i - 1)
                    dve.tensor_tensor(x2[:], ps[:, 3, :], x_nat[1 - p][:], ALU.add).then_inc(x2_ready, 1)
                    dve.wait_ge(x3t_hi, i)
                    dve.tensor_tensor(x3t_l[:], ps[:, 6, :].rearrange("p (c n) -> p c n", c=KC),
                                      x3t_h[:].bitcast(F32), ALU.subtract).then_inc(x3t_lo, 1)

            pipelined(dve, iteration)

        @block.tensor
        def _(pe):
            def product(out_ap, a_h, a_l, b_h, b_l, start, stop):
                pe.matmul(out_ap, a_h, b_h, start=start, stop=False)
                pe.matmul(out_ap, a_h, b_l, start=False, stop=False)
                return pe.matmul(out_ap, a_l, b_h, start=False, stop=stop)

            pe.wait_ge(set_up, 2)
            pe.matmul(ps[:, 0, 0:NA], const("before"), onehot[:], start=True, stop=True)
            pe.matmul(ps[:, 0, NA:2 * NA], const("ones"), onehot[:], start=True, stop=True).then_inc(route_ps, 1)
            pe.wait_ge(set_up, MATCH_STEP)
            pe.matmul(ps[0:1, 1, 0:NSLOT], const("sample"), match, start=True, stop=True).then_inc(route_ps, 1)
            for j in range(SPT):
                q = slice(j * T, (j + 1) * T)
                pe.matmul(ps[q, 2, 0:ST], const("sample_row"), match[:, j:NSLOT:SPT], start=True, stop=True)
                last = pe.matmul(ps[q, 2, ST:2 * ST], const("ones")[:, 0:T], match[:, j:NSLOT:SPT], start=True, stop=True)
            last.then_inc(route_ps, 1)
            for j in range(SPT):
                last = pe.matmul(ps[j * T:(j + 1) * T, 3, 0:NT], const("ones")[0:1, 0:T], idsm_f[0:1, j:NB:SPT],
                                 start=True, stop=True)
            last.then_inc(route_ps, 1)

            def adapters(i):
                return numbers(mybir.EngineType.PE, tile_adapter[0:1, bass.ds(i * XB, XB)], NA - 1)

            def adapter_product(i, u, a, again):
                pe.wait_ge(w_ready, a + 1)
                pe.wait_ge(xt_ready, i * XB + u + 1)
                if again:
                    pe.wait_ge(y_copied, i * XB + (u - XB + 1))
                for c in range(KC):
                    last = pe.matmul(ps[:, 4 + u, :], xt_sb[u % 2][:, c].rearrange("p s t -> p (s t)"),
                                     w_all[:, bass.ds(a, 1), c, :], start=(c == 0), stop=(c == KC - 1))
                last.then_inc(y_ps, 1)

            pe.wait_ge(routed, 1)
            for u, a in enumerate(adapters(0)):
                adapter_product(0, u, a, False)
            with pe.Fori(1, ST // XB) as i:
                for u, a in enumerate(adapters(i)):
                    adapter_product(i, u, a, True)

            pe.wait_ge(wqkv_lo, 1)
            pe.wait_ge(y_copied, ST)
            pe.wait_ge(mix_ready, SPT)

            def y_transpose(t, p, k):
                if has(t):
                    pe.wait_ge(y_in[p], k * 16 + 16)
                    need(pe, cxt_lo, t - 2)
                    for c in range(KC):
                        last = pe.transpose(ps[:, 0, c * P:(c + 1) * P], y_nat[p][:, c * P:(c + 1) * P], ident)
                    last.then_inc(yt_ps, 1)

            y_transpose(0, 0, 0)

            causal = causal_bf[:].rearrange("p (h t) -> p h t", h=1).broadcast_to([P, 2 * KV, T])

            def scores(half):
                pe.matmul(ps[:, 3 + half, :], ident_bf[:], causal, start=True, stop=False)
                for s in range(2 * half, 2 * half + 2):
                    n = (s % 2) * KV * T
                    last = pe.matmul(ps[:, 3 + half, n:n + KV * T], qt[:, s, :], k_bd[:, s].rearrange("p h t -> p (h t)"),
                                     start=False, stop=(s % 2 == 1))
                return last

            def dense(c):
                for bank, n in ((7, 0), (5, NFH)):
                    last = product(ps[:, bank, 0:NFH], x3t_h[:, c, :], x3t_l[:, c, :],
                                   wf_h[:, c, n:n + NFH], wf_l[:, c, n:n + NFH], c == 0, c == KC - 1)
                return last

            def iteration(i, p, k):
                if has(i):
                    pe.wait_ge(yt_lo, i + 1)
                    need(pe, qt_ready, i)
                    need(pe, k_ready, i)
                    for c in range(KC):
                        a_h, a_l = yt_h[:, c, :], yt_l[:, c, :]
                        product(ps[:, 1, :], a_h, a_l, wqkv_h[:, c, 0:NQ], wqkv_l[:, c, 0:NQ], c == 0, c == KC - 1)
                        last = product(ps[:, 2, 0:2 * NKV], a_h, a_l, wqkv_h[:, c, NQ:NQKV], wqkv_l[:, c, NQ:NQKV],
                                       c == 0, c == KC - 1)
                    last.then_inc(qkv_ps, 1)
                if has(i - 3):
                    pe.wait_ge(hw_ready, i - 2)
                    need(pe, x3t_lo, min(i - 1, NT) if isinstance(i, int) else i - 1)
                    pe.transpose(ps[:, 6, 0:P], hw[:].rearrange("p e r -> p (e r)"), ident).then_inc(hwt_ps, 1)
                y_transpose(i + 1, 1 - p, k + p if not isinstance(i, int) else (i + 1) // 2)
                if has(i - 1):
                    pe.wait_ge(exp_ready, i)
                    for h in range(KV):
                        n = (h % 4) * P
                        last = pe.transpose(ps[:, 3 + h // 4, n:n + P], prob[:, h].rearrange("p s t -> p (s t)"), ident)
                    last.then_inc(pt_ps, 1)
                if has(i - 3):
                    pe.wait_ge(hwt_ready, i - 2)
                    pe.matmul(ps[:, 7, 0:NFH], hwt[:], wb_sb[:, 0:NFH], start=False, stop=True, skip_group_check=True)
                    pe.matmul(ps[:, 5, 0:D - NFH], hwt[:], wb_sb[:, NFH:D], start=False, stop=True,
                              skip_group_check=True).then_inc(out_ps, 1)
                if has(i - 1):
                    pe.wait_ge(pt_lower, i)
                    pe.wait_ge(pt_upper, i)
                    pe.wait_ge(v_ready, i)
                    for h in range(KV):
                        n = (h % 4) * P
                        last = pe.matmul(ps[:, 3 + h // 4, n:n + SPT * VW], pt[:, h, :],
                                         v_bd[1 - p][:, h].rearrange("p s w -> p (s w)"), start=True, stop=True)
                    last.then_inc(cx_ps, 1)
                if has(i):
                    pe.wait_ge(roped, i + 1)
                    pe.wait_ge(v_ready, i + 1)
                    for g in range(G):
                        pe.transpose(ps[:, 1, g * P:(g + 1) * P], qk[:, g * P:(g + 1) * P], ident)
                    pe.transpose(ps[:, 2, 0:P], qk[:, NQ:NQK], ident).then_inc(qkt_ps, 1)
                if has(i - 2):
                    pe.wait_ge(x3t_lo, i - 1)
                    need(pe, out_ready, i - 2)
                    dense(0)
                if has(i - 1):
                    pe.wait_ge(cx_ready, i)
                    need(pe, yt_lo, min(i + 2, NT) if isinstance(i, int) else i + 2)
                    for s in range(SPT):
                        last = pe.transpose(ps[:, 0, s * P:(s + 1) * P], cx[:, s].rearrange("p h d -> p (h d)"), ident)
                    last.then_inc(cxt_ps, 1)
                if has(i - 2):
                    for c in range(1, KC):
                        last = dense(c)
                    last.then_inc(h_ps, 1)
                if isinstance(i, int) and i == 1:
                    pe.wait_ge(w2_lo, 1)
                if has(i - 1):
                    pe.wait_ge(cxt_lo, i)
                    for g in range(G):
                        last = product(ps[:, 3, :], cxt_h[:, g].rearrange("p s t -> p (s t)"),
                                       cxt_l[:, g].rearrange("p s t -> p (s t)"), wo_h[:, g, :], wo_l[:, g, :],
                                       g == 0, g == G - 1)
                    last.then_inc(wo_ps, 1)
                if has(i):
                    pe.wait_ge(qt_ready, i + 1)
                    pe.wait_ge(k_ready, i + 1)
                    scores(1)
                if has(i - 1):
                    pe.wait_ge(x2_ready, i)
                    need(pe, hwt_ready, i - 3)
                    mix = mix_bd[:, i - 1, :] if isinstance(i, int) else \
                        mix_bd[:, bass.ds(i - 1, 1), :].rearrange("p a n -> p (a n)")
                    for c in range(KC):
                        last = pe.matmul(ps[:, 6, c * P:(c + 1) * P], x2[:, c * P:(c + 1) * P], mix, start=True, stop=True)
                    last.then_inc(x3t_ps, 1)
                if has(i):
                    scores(0).then_inc(scores_ps, 1)

            pipelined(pe, iteration)


MATCH_STEP = 13
MIX_FROM = 2


def kernel(x, itok_B_1_14, itok_B_0_15, L0_cond_weight, L0_attn_Wq, L0_attn_Wk, L0_attn_Wv, L0_attn_Wo,
           L0_cond2_weights, L0_ffn_W_base, L0_ffn_b_base, L0_ffn_W_gate, L0_ffn_A, L0_ffn_B):
    import concourse.bacc as bacc
    from concourse.bass_utils import run_bass_kernel_spmd

    def chunked(w):
        return w.reshape(KC, P, w.shape[1]).transpose(1, 0, 2)

    a = np.asarray
    x = a(x)
    consts, where = constants()
    wq = a(L0_attn_Wq).reshape(D, KV, G, HD).transpose(0, 2, 1, 3).reshape(D, NQ)
    arrays = {
        "x": x.reshape(NB * T, D),
        "xt": x.reshape(NB, T, KC, P).transpose(0, 3, 2, 1).reshape(NB * P, KC * T),
        "ids_a": a(itok_B_1_14),
        "ids_m": a(itok_B_0_15),
        "wcond": a(L0_cond_weight).transpose(0, 2, 1).reshape(NA, KC, P, D).transpose(0, 2, 1, 3),
        "wqkv": chunked(np.concatenate([wq, a(L0_attn_Wk), a(L0_attn_Wv)], 1)),
        "wo": a(L0_attn_Wo).reshape(KV, G, HD, D).transpose(0, 2, 1, 3).reshape(P, G, D),
        "wmix": a(L0_cond2_weights).reshape(NA * T, T),
        "wffn": chunked(np.concatenate([a(L0_ffn_W_base).T, a(L0_ffn_A).reshape(ER, D).T, a(L0_ffn_W_gate).T], 1)),
        "wb": a(L0_ffn_B).transpose(0, 2, 1).reshape(ER, D),
        "bias": a(L0_ffn_b_base),
        "consts": consts,
    }
    arrays = {name: np.ascontiguousarray(v) for name, v in arrays.items()}
    nc = bacc.Bacc("TRN2", target_bir_lowering=False, num_devices=1)
    args = [nc.dram_tensor(name, v.shape, mybir.dt.from_np(v.dtype), kind="ExternalInput").ap()
            for name, v in arrays.items()]
    out = nc.dram_tensor("out", (NB * T, D), F32, kind="ExternalOutput").ap()
    build(nc, *args, out, where)
    result = run_bass_kernel_spmd(nc, [arrays], core_ids=[0])
    return result.results[0]["out"].reshape(NB, T, D)
```

```python
from contextlib import ExitStack

import numpy as np

import concourse.bass as bass
from concourse import mybir

F32 = mybir.dt.float32
F32R = mybir.dt.float32r
BF16 = mybir.dt.bfloat16
I32 = mybir.dt.int32
U32 = mybir.dt.uint32
ALU = mybir.AluOpType
ACT = mybir.ActivationFunctionType
X = mybir.AxisListType.X

P = 128
NB, T, D = 128, 32, 512
KC = D // P
NA = 16
SPT = P // T
NT = NB // SPT
ST = (NB + NA * (SPT - 1)) // SPT
NSLOT = ST * SPT
KV, G, HD = 8, 4, 16
HALF = HD // 2
NQ, NKV = KV * G * HD, KV * HD
NQK = NQ + NKV
NQKV = NQ + 2 * NKV
E, R = 8, 16
ER = E * R
NF = D + ER + E
NFH = NF // 2
VW = HD + 1
XB = 4
NEG = -1.0e30
ROPE_BASE = 500000.0


def constants():
    p = np.arange(P)
    slot = np.arange(NSLOT)
    inv = (1.0 / ROPE_BASE ** (np.arange(0, HD, 2, dtype=np.float32) / HD)).astype(np.float32)
    angle = ((p % T).astype(np.float32)[:, None] * inv[None, :]).astype(np.float32)
    cos, sin = np.cos(angle), np.sin(angle)
    rows = np.ones((P, 1))
    a = np.arange(NA)
    parts = {
        "ident": np.eye(P),
        "cos": np.concatenate([cos, cos], 1),
        "sin": np.concatenate([-sin, sin], 1),
        "kvmask": (p[:, None] // HD == np.arange(KV)[None, :]),
        "own_sample": (p[:, None] // T == np.arange(SPT)[None, :]),
        "before": (p[:, None] < p[None, :]),
        "ones": np.ones((P, P)),
        "causal": np.where(np.arange(T)[None, :] > (p % T)[:, None], NEG, 0.0),
        "iota_a": rows * a,
        "rev_e": rows * (E - np.arange(E)),
        "four_m": rows * (SPT * np.arange(NB // SPT)),
        "upto": rows * (a[None, :] <= a[:, None]).reshape(1, -1),
        "iota_slot": rows * slot,
        "iota_tile": rows * np.arange(ST),
        "sample": p[:, None],
        "sample_row": np.repeat(p[:, None] * T, T, 1),
        "pad_row": (NB + SPT * np.arange(ST)[None, :] + p[:, None] // T) * T,
        "token": p[:, None] % T,
    }
    at, where = 0, {}
    for name, v in parts.items():
        where[name] = (at, v.shape[1])
        at += v.shape[1]
    return np.ascontiguousarray(np.concatenate([np.asarray(v, np.float32) for v in parts.values()], 1)), where


def build(nc, x, xt, ids_a, ids_m, wcond, wqkv, wo, wmix, wffn, wb, bias, consts, out, where):
    ncols = consts.shape[1]
    with ExitStack() as ctx:
        def sb(name, shape, dt=F32):
            return ctx.enter_context(nc.sbuf_tensor(name, shape, dt))

        def sem(name):
            return ctx.enter_context(nc.semaphore(name))

        ps = ctx.enter_context(nc.psum_tensor("ps", [P, 8, 512], F32))
        y_rows = nc.dram_tensor("y_rows", ((NB + NSLOT) * T, D), F32, kind="Internal").ap()

        cst = sb("cst", [P, ncols])

        def const(name):
            a, n = where[name]
            return cst[:, a:a + n]

        ident = const("ident")
        ident_bf = sb("ident_bf", [P, P], BF16)
        causal_bf = sb("causal_bf", [P, T], BF16)
        wqkv_h = sb("wqkv_h", [P, KC, NQKV], F32R)
        wqkv_l = sb("wqkv_l", [P, KC, NQKV], F32R)
        mix_bd = sb("mix_bd", [P, NT, P])

        stage1 = ExitStack()
        def sb1(name, shape, dt=F32):
            return stage1.enter_context(nc.sbuf_tensor(name, shape, dt))
        w_all = sb1("w_all", [P, NA, KC, D])
        xt_raw = [sb1(f"xt_raw{u}", [P, SPT, KC, T]) for u in range(XB)]
        xt_sb = [sb1(f"xt_sb{p}", [P, KC, SPT, T]) for p in range(2)]
        y_sb = [sb1(f"y_sb{u}", [P, D]) for u in range(2)]
        wqkv_raw = sb1("wqkv_raw", [P, KC, NQKV])
        wide = w_all[:, NA - 1].rearrange("p c n -> p (c n)")
        mix_own = wqkv_raw[:].rearrange("p c n -> p (c n)")[:, 0:NT * T].rearrange("p (g d) -> p g d", d=T)
        mix_sum = wqkv_raw[:].rearrange("p c n -> p (c n)")[:, NT * T:2 * NT * T].rearrange("p (g d) -> p g d", d=T)
        wmix_sb = sb1("wmix_sb", [P, NA, T])
        ids_mix = sb1("ids_mix", [P, NT])
        idsm_f = sb1("idsm_f", [1, NB])
        ids_col = sb1("ids_col", [P, 1], I32)
        idsm_row = sb1("idsm_row", [1, NB], I32)
        idsf = sb1("idsf", [P, 1])
        onehot = sb1("onehot", [P, NA])
        tiles_a = sb1("tiles_a", [P, NA])
        end_a = sb1("end_a", [P, NA])
        base_a = sb1("base_a", [P, NA])
        pos_a = sb1("pos_a", [P, NA])
        pos = sb1("pos", [P, 1])
        match = wide[:, 0:NSLOT]
        adapter_f = sb1("adapter_f", [P, ST])
        tile_adapter = sb1("tile_adapter", [P, ST], I32)
        slot_sample = sb1("slot_sample", [1, NSLOT], I32)
        pad = wide[:, NSLOT:NSLOT + ST]
        y_row = sb1("y_row", [P, ST], U32)
        stage1.close()

        wo_raw = sb("wo_raw", [P, G, D])
        wo_h = sb("wo_h", [P, G, D], F32R)
        wo_l = sb("wo_l", [P, G, D], F32R)
        wf_raw = sb("wf_raw", [P, KC, NF])
        wf_h = sb("wf_h", [P, KC, NF], F32R)
        wf_l = sb("wf_l", [P, KC, NF], F32R)
        wb_sb = sb("wb_sb", [P, D])
        bias_sb = sb("bias_sb", [P, D])
        FREED = 8
        assert (3 * (G * D + KC * NF) + 2 * D) <= FREED * KC * D
        LAST_USE = (NB + FREED * (SPT - 1)) // SPT
        y_nat = [sb(f"y_nat{p}", [P, D]) for p in range(2)]
        x_nat = [sb(f"x_nat{p}", [P, D]) for p in range(2)]
        yt_h = sb("yt_h", [P, KC, P], F32R)
        yt_l = sb("yt_l", [P, KC, P], F32R)
        rope_a = sb("rope_a", [P, NQK])
        rope_b = sb("rope_b", [P, NQK])
        qk = sb("qk", [P, NQK])
        v_bd = [sb(f"v_bd{p}", [P, KV, SPT, VW]) for p in range(2)]
        qt_h = sb("qt_h", [P, SPT, P], F32R)
        qt_l = sb("qt_l", [P, SPT, P], F32R)
        kt_h = sb("kt_h", [P, SPT, T], F32R)
        kt_l = sb("kt_l", [P, SPT, T])
        k_bd_h = sb("k_bd_h", [P, SPT, KV, T], F32R)
        k_bd_l = sb("k_bd_l", [P, SPT, KV, T], F32R)
        row_max = sb("row_max", [P, SPT * KV])
        prob = sb("prob", [P, KV, SPT, T])
        pt = sb("pt", [P, KV, P])
        recip = sb("recip", [P, KV, SPT])
        cx = sb("cx", [P, SPT, KV, HD])
        cxt_h = sb("cxt_h", [P, G, SPT, T], F32R)
        cxt_l = sb("cxt_l", [P, G, SPT, T], F32R)
        x2 = sb("x2", [P, D])
        x2b = [sb(f"x2b{p}", [P, D]) for p in range(2)]
        x3t_h = sb("x3t_h", [P, KC, P], F32R)
        x3t_l = sb("x3t_l", [P, KC, P], F32R)
        logit = sb("logit", [P, E])
        logit2 = sb("logit2", [P, E])
        first = sb("first", [P, E])
        second = sb("second", [P, E])
        pick = sb("pick", [P, E])
        route = sb("route", [P, E])
        rs = sb("rs", [P, 8])
        hw = sb("hw", [P, E, R])
        hwt = sb("hwt", [P, P])
        o_sb = [sb(f"o_sb{p}", [P, D]) for p in range(2)]

        cst_in = sem("cst_in")
        ids_in = sem("ids_in")
        w_in = [sem(f"w_in{a}") for a in range(NA)]
        wqkv_in = sem("wqkv_in")
        xt_in = [sem(f"xt_in{u}") for u in range(XB)]
        wmix_in = sem("wmix_in")
        mix_part = sem("mix_part")
        mix_added = sem("mix_added")
        mix_ready = sem("mix_ready")
        w2_in = sem("w2_in")
        y_in = [sem(f"y_in{p}") for p in range(2)]
        x_in = [sem(f"x_in{p}") for p in range(2)]
        set_up = sem("set_up")
        route_ps = sem("route_ps")
        routed = sem("routed")
        w_ready = sem("w_ready")
        xt_ready = sem("xt_ready")
        y_ps = sem("y_ps")
        y_copied = sem("y_copied")
        y_stored = [sem(f"y_stored{u}") for u in range(2)]
        zeroed = sem("zeroed")
        wqkv_hi = sem("wqkv_hi")
        wqkv_lo = sem("wqkv_lo")
        w2_hi = sem("w2_hi")
        w2_lo = sem("w2_lo")
        yt_ps, yt_hi, yt_lo = sem("yt_ps"), sem("yt_hi"), sem("yt_lo")
        qkv_ps, roped_parts, roped, v_ready = sem("qkv_ps"), sem("roped_parts"), sem("roped"), sem("v_ready")
        qkt_ps, kt_hi, kt_lo, qt_hi, qt_lo = sem("qkt_ps"), sem("kt_hi"), sem("kt_lo"), sem("qt_hi"), sem("qt_lo")
        k_bd_hi, k_bd_lo = sem("k_bd_hi"), sem("k_bd_lo")
        scores_ps, max_ready = sem("scores_ps"), sem("max_ready")
        shifted, exp_ready = sem("shifted"), sem("exp_ready")
        masked = sem("masked")
        pt_ps, pt_ready = sem("pt_ps"), sem("pt_ready")
        cx_ps, recip_ready, cx_ready = sem("cx_ps"), sem("recip_ready"), sem("cx_ready")
        cxt_ps, cxt_hi, cxt_lo = sem("cxt_ps"), sem("cxt_hi"), sem("cxt_lo")
        wo_ps, x2_ready, x2b_ready = sem("wo_ps"), sem("x2_ready"), sem("x2b_ready")
        x3t_ps, x3t_hi, x3t_lo = sem("x3t_ps"), sem("x3t_hi"), sem("x3t_lo")
        h_ps, route_step, gate_exp = sem("h_ps"), sem("route_step"), sem("gate_exp")
        hw_ready, hwt_ps, hwt_ready = sem("hw_ready"), sem("hwt_ps"), sem("hwt_ready")
        out_ps, out_ready = sem("out_ps"), sem("out_ready")
        out_stored = [sem(f"out_stored{p}") for p in range(2)]

        RSTEPS = 12

        def need(eng, s, n):
            if not isinstance(n, int) or n > 0:
                eng.wait_ge(s, n)

        def numbers(engine, ap, top):
            return nc.values_load_multi_w_load_instructions(ap, engines=[engine], min_val=0, max_val=top)[1]

        def has(t):
            return not isinstance(t, int) or 0 <= t < NT

        def pipelined(eng, iteration, ahead=1):
            for i in range(4):
                iteration(i, i % 2, i // 2)
            with eng.Fori(2, NT // 2 - ahead) as k:
                for u in range(2):
                    iteration(k * 2 + u, u, k)
            for i in range(NT - 2 * ahead, NT + 3):
                iteration(i, i % 2, i // 2)

        block = ctx.enter_context(nc.Block())

        @block.sync
        def _(sp):
            sp.dma_start(ids_col[:], ids_a.rearrange("(p a) -> p a", a=1)).then_inc(ids_in, 16)
            sp.dma_start(idsm_row[:], ids_m.rearrange("(a p) -> a p", a=1)).then_inc(ids_in, 16)
            sp.dma_start(cst[:], consts).then_inc(cst_in, 16)
            sp.wait_ge(routed, 1)

            def gather(i, again):
                regs = []
                for u in range(XB):
                    if u % 2 == 0:
                        regs = numbers(mybir.EngineType.SP,
                                       slot_sample[0:1, bass.ds((i * XB + u) * SPT, 2 * SPT)], NB - 1)
                    for j in range(SPT):
                        if again and j == 0:
                            sp.wait_ge(xt_ready, i * XB + (u - XB + 1))
                        sp.dma_start(xt_raw[u][:, j].rearrange("p c t -> p (c t)"),
                                     xt[bass.ds(regs[u % 2 * SPT + j] * P, P), :]).then_inc(xt_in[u], 16)

            gather(0, False)
            for j in range(SPT):
                sp.dma_start(wmix_sb[j * T:(j + 1) * T], wmix.rearrange("(a c) d -> c a d", a=NA)).then_inc(wmix_in, 16)
            with sp.Fori(1, ST // XB) as i:
                gather(i, True)

            sp.wait_ge(y_ps, ST)
            sp.wait_ge(y_copied, ST)
            sp.wait_ge(mix_ready, SPT)
            sp.wait_ge(wqkv_lo, KC)
            for u in range(2):
                sp.wait_ge(y_stored[u], 16 * (ST // 2))

            def rows(t):
                return bass.ds(t * P, P)

            def load_y(t, p):
                if has(t):
                    need(sp, yt_ps, t - 1)
                    sp.dma_start(y_nat[p][:], y_rows[rows(t), :]).then_inc(y_in[p], 16)

            def load_x(t, p):
                if has(t):
                    need(sp, x2_ready, 2 * (t - 1))
                    sp.dma_start(x_nat[p][:], x[rows(t), :]).then_inc(x_in[p], 16)

            load_y(0, 0)
            load_y(1, 1)
            load_x(0, 0)
            load_y(2, 0)

            def iteration(i, p, k):
                load_y(i + 3, 1 - p)
                if has(i - 3):
                    sp.wait_ge(out_ready, i - 2)
                    sp.dma_start(out[rows(i - 3), :], o_sb[1 - p][:]).then_inc(out_stored[1 - p], 16)
                load_x(i + 1, 1 - p)

            pipelined(sp, iteration, ahead=2)
            for p in range(2):
                sp.wait_ge(out_stored[p], 16 * (NT // 2))

        @block.gpsimd
        def _(pool):
            pool.memset(mix_bd[:], 0.0).then_inc(zeroed, 1)

            def store_y(t):
                pool.wait_ge(y_copied, t + 1)
                pool.indirect_dma_start(y_rows[:, :], bass.IndirectOffsetOnAxis(ap=y_row[:, t:t + 1], axis=0),
                                        y_sb[t % 2][:], None).then_inc(y_stored[t % 2], 16)

            pool.wait_ge(routed, 3)
            for t in range(ST):
                store_y(t)
                if t == MIX_FROM:
                    pool.wait_ge(wqkv_lo, KC)
                    pool.memset(mix_sum, 0.0).then_inc(mix_added, 1)
                if t > MIX_FROM and (t - MIX_FROM) % 2 == 0 and (t - MIX_FROM) // 2 <= NA:
                    n = (t - MIX_FROM) // 2
                    pool.wait_ge(mix_part, n)
                    pool.wait_ge(mix_added, n)
                    pool.tensor_tensor(mix_sum, mix_sum, mix_own, ALU.add).then_inc(mix_added, 1)

            pool.wait_ge(y_ps, ST)
            for u in range(2):
                pool.wait_ge(y_stored[u], 16 * (ST // 2))
            pool.wait_ge(mix_ready, SPT)
            pool.wait_ge(wqkv_lo, KC)
            for p in range(2):
                pool.memset(v_bd[p][:], 0.0).then_inc(zeroed, 1)
            pool.wait_ge(zeroed, 3)
            for p in range(2):
                pool.tensor_copy(v_bd[p][:, :, :, HD], const("own_sample").rearrange("p (h s) -> p h s", h=1)
                                 .broadcast_to([P, KV, SPT])).then_inc(zeroed, 1)

            def iteration(i, p, k):
                if has(i):
                    pool.wait_ge(roped_parts, i + 1)
                    need(pool, qkt_ps, i)
                    pool.tensor_tensor(qk[:], rope_a[:], rope_b[:], ALU.add).then_inc(roped, 1)
                if has(i - 1):
                    if isinstance(i, int) and i == 1:
                        pool.wait_ge(w2_in, 80)
                    pool.wait_ge(x2_ready, 2 * i)
                    need(pool, out_ready, i - 2)
                    pool.tensor_tensor(x2b[1 - p][:], x2[:], bias_sb[:], ALU.add).then_inc(x2b_ready, 1)

            pipelined(pool, iteration)

        @block.scalar
        def _(act):
            act.wait_ge(ids_in, 32)
            for a in range(NA):
                if a >= 2:
                    act.wait_ge(w_in[a - 1], 16)
                    act.sem_inc(w_ready, 1)
                if a == NA - 1:
                    act.wait_ge(route_ps, 4)
                    act.wait_ge(routed, 3)
                act.dma_start(w_all[:, a], wcond[a]).then_inc(w_in[a], 16)
                if a == 1:
                    act.wait_ge(w_in[0], 16)
                    act.sem_inc(w_ready, 1)
                if a == WQKV_AT:
                    act.wait_ge(w_in[a], 16)
                    act.dma_start(wqkv_raw[:], wqkv).then_inc(wqkv_in, 16)
                    act.wait_ge(wqkv_in, 16)
                if a == WQKV_AT + 1:
                    act.activation(wqkv_h[:], wqkv_raw[:], ACT.Copy).then_inc(wqkv_hi, 1)
            act.wait_ge(w_in[NA - 1], 16)
            act.sem_inc(w_ready, 1)

            act.wait_ge(y_ps, LAST_USE)
            act.dma_start(wo_raw[:], wo).then_inc(w2_in, 16)
            for c in range(0, KC, 2):
                act.wait_ge(w2_in, 16 + 8 * c)
                act.dma_start(wf_raw[:, c:c + 2], wffn[:, c:c + 2]).then_inc(w2_in, 16)
            act.wait_ge(w2_in, 48)
            act.dma_start(wb_sb[:], wb).then_inc(w2_in, 16)
            act.dma_start(bias_sb[:], bias.rearrange("(a d) -> a d", a=1).broadcast_to([P, D])).then_inc(w2_in, 16)

            act.wait_ge(zeroed, 1)
            act.wait_ge(mix_added, NA + 1)
            for j in range(SPT):
                q = slice(j * T, (j + 1) * T)
                act.activation(mix_bd[q, :, q], mix_sum[q], ACT.Copy).then_inc(mix_ready, 1)
            act.wait_ge(w2_in, 80)
            act.activation(wo_h[:], wo_raw[:], ACT.Copy)
            act.activation(wf_h[:], wf_raw[:], ACT.Copy).then_inc(w2_hi, 1)

            act.wait_ge(y_ps, ST)
            for u in range(2):
                act.wait_ge(y_stored[u], 16 * (ST // 2))
            act.wait_ge(mix_ready, SPT)
            act.wait_ge(wqkv_lo, KC)

            def split_hi(t):
                if has(t):
                    act.wait_ge(yt_ps, t + 1)
                    need(act, qkv_ps, t)
                    act.activation(yt_h[:], ps[:, 0, :].rearrange("p (c n) -> p c n", c=KC), ACT.Copy).then_inc(yt_hi, 1)

            def exponentials(t, half):
                act.wait_ge(shifted, 2 * t + 2 - half)
                e = prob[:, :, 2 * half:2 * half + 2, :]
                act.activation(e, e, ACT.Exp, scale=HD ** -0.5).then_inc(exp_ready, 1)

            split_hi(0)

            def iteration(i, p, k):
                if has(i - 1):
                    exponentials(i - 1, 0)
                if has(i - 3):
                    act.wait_ge(hwt_ps, i - 2)
                    need(act, out_ps, i - 3)
                    act.activation(hwt[:], ps[:, 6, 0:P], ACT.Copy).then_inc(hwt_ready, 1)
                if has(i - 1):
                    act.wait_ge(pt_ps, i)
                    need(act, cx_ps, i - 1)
                    for half in range(2):
                        act.activation(pt[:, half * KV // 2:(half + 1) * KV // 2],
                                       ps[:, 3 + half, :].rearrange("p (h n) -> p h n", h=KV // 2),
                                       ACT.Copy).then_inc(pt_ready, 1)
                split_hi(i + 1)
                if has(i):
                    act.wait_ge(roped_parts, i + 1)
                    if isinstance(i, int) and i == 0:
                        act.wait_ge(zeroed, 5)
                    need(act, cx_ps, i - 1)
                    for j in range(SPT):
                        q = slice(j * T, (j + 1) * T)
                        last = act.activation(v_bd[p][q, :, j, 0:HD],
                                              ps[q, 2, NKV:2 * NKV].rearrange("p (h d) -> p h d", h=KV), ACT.Copy)
                    last.then_inc(v_ready, 1)
                    act.wait_ge(qkt_ps, i + 1)
                    need(act, scores_ps, 2 * i)
                    need(act, k_bd_lo, i)
                    act.activation(kt_h[:], ps[:, 2, 0:P].rearrange("p (s t) -> p s t", s=SPT), ACT.Copy).then_inc(kt_hi, 1)
                    act.activation(qt_h[:].rearrange("p s (g t) -> p s g t", g=G),
                                   ps[:, 1, :].rearrange("p (g s t) -> p s g t", s=SPT, g=G), ACT.Copy).then_inc(qt_hi, 1)
                if has(i - 1):
                    act.wait_ge(cxt_ps, i)
                    need(act, wo_ps, i - 1)
                    act.activation(cxt_h[:].rearrange("p g s t -> p s g t"),
                                   ps[:, 0, :].rearrange("p (s g t) -> p s g t", s=SPT, g=G), ACT.Copy).then_inc(cxt_hi, 1)
                if has(i):
                    act.wait_ge(kt_hi, i + 1)
                    for h in range(KV):
                        last = act.activation(k_bd_h[:, :, h, :], kt_h[:].bitcast(F32), ACT.Copy,
                                              scale=const("kvmask")[:, h:h + 1])
                    last.then_inc(k_bd_hi, 1)
                if has(i - 2):
                    act.wait_ge(route_step, (i - 2) * RSTEPS + 7)
                    act.activation(rs[:, 4:5], rs[:, 0:1], ACT.Exp, bias=rs[:, 2:3], scale=-1.0).then_inc(gate_exp, 1)
                if has(i - 1):
                    act.wait_ge(x3t_ps, i)
                    need(act, h_ps, i - 1)
                    act.activation(x3t_h[:], ps[:, 6, :].rearrange("p (c n) -> p c n", c=KC), ACT.Copy).then_inc(x3t_hi, 1)
                if has(i):
                    exponentials(i, 1)

            pipelined(act, iteration)

        @block.vector
        def _(dve):
            steps = [0]

            def then(ins):
                steps[0] += 1
                ins.then_inc(set_up, 1)
                dve.wait_ge(set_up, steps[0])

            dve.wait_ge(ids_in, 32)
            dve.tensor_copy(idsm_f[:], idsm_row[:])
            then(dve.tensor_copy(idsf[:], ids_col[:]))
            dve.wait_ge(cst_in, 16)
            then(dve.tensor_scalar(onehot[:], const("iota_a"), idsf[:, 0:1], None, ALU.is_equal))
            dve.tensor_copy(ident_bf[:], ident)
            dve.tensor_copy(causal_bf[:], const("causal"))
            dve.wait_ge(route_ps, 1)
            wide_m = wide[:, 0:NA * NT].rearrange("p (a m) -> p a m", a=NA)
            count = ps[:, 0, NA:2 * NA].rearrange("p (a m) -> p a m", m=1).broadcast_to([P, NA, NT])
            four = const("four_m").rearrange("p (a m) -> p a m", a=1).broadcast_to([P, NA, NT])
            then(dve.tensor_tensor(wide_m, count, four, ALU.is_gt))
            then(dve.tensor_reduce(tiles_a[:], wide_m, X, ALU.add))
            wide_a = wide[:, 0:NA * NA].rearrange("p (a b) -> p a b", a=NA)
            upto = const("upto").rearrange("p (a b) -> p a b", a=NA)
            then(dve.tensor_tensor(wide_a, upto, tiles_a[:].rearrange("p (a b) -> p a b", a=1).broadcast_to([P, NA, NA]),
                                   ALU.mult))
            then(dve.tensor_reduce(end_a[:], wide_a, X, ALU.add))
            then(dve.tensor_tensor(base_a[:], end_a[:], tiles_a[:], ALU.subtract))
            then(dve.scalar_tensor_tensor(pos_a[:], base_a[:], float(SPT), ps[:, 0, 0:NA], ALU.mult, ALU.add))
            then(dve.tensor_tensor(pos_a[:], pos_a[:], onehot[:], ALU.mult))
            then(dve.tensor_reduce(pos[:], pos_a[:], X, ALU.add))
            then(dve.tensor_scalar(match, const("iota_slot"), pos[:, 0:1], None, ALU.is_equal))
            assert steps[0] == MATCH_STEP
            dve.wait_ge(route_ps, 2)
            dve.tensor_copy(slot_sample[:], ps[0:1, 1, 0:NSLOT]).then_inc(routed, 1)
            wide_t = wide[:, NSLOT + ST:NSLOT + ST + ST * NA].rearrange("p (t a) -> p t a", a=NA)
            tile_no = const("iota_tile").rearrange("p (t a) -> p t a", a=1).broadcast_to([P, ST, NA])
            then(dve.tensor_tensor(wide_t, tile_no, end_a[:].rearrange("p (t a) -> p t a", t=1).broadcast_to([P, ST, NA]),
                                   ALU.is_ge))
            then(dve.tensor_reduce(adapter_f[:], wide_t, X, ALU.add))
            dve.tensor_scalar(tile_adapter[:], adapter_f[:], float(NA - 1), None, ALU.min).then_inc(routed, 1)
            dve.wait_ge(route_ps, 3)
            then(dve.tensor_scalar(pad, ps[:, 2, ST:2 * ST], -1.0, 1.0, ALU.mult, ALU.add))
            then(dve.tensor_tensor(pad, pad, const("pad_row"), ALU.mult))
            then(dve.tensor_tensor(pad, ps[:, 2, 0:ST], pad, ALU.add))
            dve.tensor_scalar(y_row[:], pad, const("token"), None, ALU.add).then_inc(routed, 1)
            dve.wait_ge(route_ps, 4)
            then(dve.tensor_copy(ids_mix[:], ps[:, 3, 0:NT]))

            def order_x(i, u, again):
                dve.wait_ge(xt_in[u], i * 64 + 64)
                if again or u >= 2:
                    dve.wait_ge(y_ps, i * XB + (u - 1))
                dve.tensor_copy(xt_sb[u % 2][:].rearrange("p c s t -> p s c t"), xt_raw[u][:]).then_inc(xt_ready, 1)

            def copy_y(i, u, again):
                dve.wait_ge(y_ps, i * XB + u + 1)
                if again or u >= 2:
                    dve.wait_ge(y_stored[u % 2], i * 32 + 16 * (u // 2))
                dve.tensor_copy(y_sb[u % 2][:], ps[:, 4 + u, :]).then_inc(y_copied, 1)

            def mix_share(a, first=False):
                if not first:
                    dve.wait_ge(mix_added, a + 1)
                dve.scalar_tensor_tensor(
                    mix_own, ids_mix[:].rearrange("p (g d) -> p g d", d=1).broadcast_to([P, NT, T]),
                    const("iota_a")[:, bass.ds(a, 1)],
                    wmix_sb[:, bass.ds(a, 1), :].broadcast_to([P, NT, T]), ALU.is_equal, ALU.mult).then_inc(mix_part, 1)

            def split_weights(c):
                if c == 0:
                    dve.wait_ge(wqkv_hi, 1)
                dve.tensor_tensor(wqkv_l[:, c], wqkv_raw[:, c], wqkv_h[:, c].bitcast(F32), ALU.subtract) \
                   .then_inc(wqkv_lo, 1)

            def slot_tiles(i, with_mix):
                for u in range(XB):
                    order_x(i if u + 1 < XB else i + 1, (u + 1) % XB, True)
                    copy_y(i, u, True)
                    if not with_mix:
                        split_weights(u)
                    elif u % 2 == 0:
                        mix_share(i * 2 + (u // 2 - 4))

            order_x(0, 0, False)
            for u in range(XB):
                if u + 1 < XB:
                    order_x(0, u + 1, False)
                else:
                    order_x(1, 0, True)
                copy_y(0, u, False)
            slot_tiles(1, False)
            dve.wait_ge(wmix_in, 16 * SPT)
            dve.wait_ge(wqkv_lo, KC)

            with dve.Fori(2, 2 + NA // 2) as i:
                slot_tiles(i, True)
            for u in range(XB):
                if u + 1 < XB:
                    order_x(ST // XB - 1, u + 1, True)
                copy_y(ST // XB - 1, u, True)

            dve.wait_ge(w2_hi, 1)
            dve.tensor_tensor(wo_l[:], wo_raw[:], wo_h[:].bitcast(F32), ALU.subtract)
            dve.tensor_tensor(wf_l[:], wf_raw[:], wf_h[:].bitcast(F32), ALU.subtract).then_inc(w2_lo, 1)

            for u in range(2):
                dve.wait_ge(y_stored[u], 16 * (ST // 2))
            dve.wait_ge(mix_ready, SPT)
            dve.wait_ge(wqkv_lo, KC)

            def split_lo(t):
                if has(t):
                    dve.wait_ge(yt_hi, t + 1)
                    dve.tensor_tensor(yt_l[:], ps[:, 0, :].rearrange("p (c n) -> p c n", c=KC),
                                      yt_h[:].bitcast(F32), ALU.subtract).then_inc(yt_lo, 1)

            split_lo(0)
            cos = const("cos").rearrange("p (h d) -> p h d", h=1).broadcast_to([P, NQK // HD, HD])
            sin = [const("sin")[:, s * HALF:(s + 1) * HALF].rearrange("p (h d) -> p h d", h=1)
                   .broadcast_to([P, NQK // HD, HALF]) for s in range(2)]
            banks12 = ps[:, 1:3, :].rearrange("p a n -> p (a n)")
            qk_ps = banks12[:, 0:NQK].rearrange("p (h d) -> p h d", d=HD)
            cxp = ps[:, 3:5, :].rearrange("p a n -> p (a n)").rearrange("p (h w) -> p h w", h=KV)[:, :, 0:SPT * VW] \
                .rearrange("p h (s w) -> p h s w", s=SPT)
            rev = const("rev_e")

            def routing(t):
                at = [0]

                def step(ins):
                    at[0] += 1
                    ins.then_inc(route_step, 1)
                    dve.wait_ge(route_step, t * RSTEPS + at[0])

                max1, key1, max2, key2, e2, den, r1, r2 = (rs[:, n:n + 1] for n in range(8))
                dve.wait_ge(h_ps, t + 1)
                step(dve.tensor_copy(logit[:], ps[:, 5, NFH - E:NFH]))
                step(dve.tensor_reduce(max1, logit[:], X, ALU.max))
                step(dve.scalar_tensor_tensor(pick[:], logit[:], max1, rev, ALU.is_equal, ALU.mult))
                step(dve.tensor_reduce(key1, pick[:], X, ALU.max))
                step(dve.tensor_scalar(first[:], rev, key1, None, ALU.is_equal))
                step(dve.scalar_tensor_tensor(logit2[:], first[:], 3.0 * NEG, logit[:], ALU.mult, ALU.add))
                step(dve.tensor_reduce(max2, logit2[:], X, ALU.max))
                step(dve.scalar_tensor_tensor(pick[:], logit2[:], max2, rev, ALU.is_equal, ALU.mult))
                dve.tensor_reduce(key2, pick[:], X, ALU.max)
                dve.wait_ge(gate_exp, t + 1)
                step(dve.tensor_scalar(den, e2, 1.0, None, ALU.add))
                dve.tensor_scalar(second[:], rev, key2, None, ALU.is_equal)
                step(dve.reciprocal(r1, den))
                dve.tensor_scalar(route[:], first[:], r1, None, ALU.mult)
                step(dve.tensor_tensor(r2, e2, r1, ALU.mult))
                step(dve.scalar_tensor_tensor(route[:], second[:], r2, route[:], ALU.mult, ALU.add))
                assert at[0] == RSTEPS
                need(dve, hwt_ps, t)
                dve.tensor_tensor(hw[:], ps[:, 5, D - NFH:NFH - E].rearrange("p (e r) -> p e r", e=E),
                                  route[:].rearrange("p (e r) -> p e r", r=1).broadcast_to([P, E, R]),
                                  ALU.mult).then_inc(hw_ready, 1)

            def shift(t, half):
                n = 2 * t + 2 - half
                row = row_max[:, half * 2 * KV:(half + 1) * 2 * KV]
                sc = ps[:, 3 + half, :].rearrange("p (h t) -> p h t", t=T)
                e = prob[:, :, 2 * half:2 * half + 2, :].rearrange("p h s t -> p s h t")
                sc = sc.rearrange("p (s h) t -> p s h t", h=KV)
                dve.wait_ge(scores_ps, n)
                need(dve, pt_ps, t)
                if half == 1:
                    mask = const("causal").rearrange("p (s h t) -> p s h t", s=1, h=1).broadcast_to([P, 2, KV, T])
                    dve.tensor_tensor(e, sc, mask, ALU.add).then_inc(masked, 1)
                    dve.wait_ge(masked, t + 1)
                    sc = e
                dve.tensor_reduce(row.rearrange("p (s h) -> p s h", h=KV), sc, X, ALU.max).then_inc(max_ready, 1)
                dve.wait_ge(max_ready, n)
                dve.tensor_tensor(e, sc, row.rearrange("p (s h t) -> p s h t", h=KV, t=1)
                                  .broadcast_to([P, 2, KV, T]), ALU.subtract).then_inc(shifted, 1)

            def iteration(i, p, k):
                if has(i - 1):
                    shift(i - 1, 0)
                if has(i - 2):
                    dve.wait_ge(x3t_hi, i - 1)
                    dve.tensor_tensor(x3t_l[:], ps[:, 6, :].rearrange("p (c n) -> p c n", c=KC),
                                      x3t_h[:].bitcast(F32), ALU.subtract).then_inc(x3t_lo, 1)
                if has(i):
                    dve.wait_ge(qkv_ps, i + 1)
                    need(dve, roped, i)
                    dve.tensor_tensor(rope_a[:].rearrange("p (h d) -> p h d", d=HD), qk_ps, cos, ALU.mult)
                    for s in range(2):
                        last = dve.tensor_tensor(
                            rope_b[:].rearrange("p (h d) -> p h d", d=HD)[:, :, s * HALF:(s + 1) * HALF],
                            qk_ps[:, :, (1 - s) * HALF:(2 - s) * HALF], sin[s], ALU.mult)
                    last.then_inc(roped_parts, 1)
                split_lo(i + 1)
                if has(i - 3):
                    dve.wait_ge(out_ps, i - 2)
                    dve.wait_ge(x2b_ready, i - 2)
                    need(dve, out_stored[1 - p], k * 16 + 16 * p - 32)
                    dve.tensor_tensor(o_sb[1 - p][:, 0:NFH], ps[:, 7, 0:NFH], x2b[1 - p][:, 0:NFH], ALU.add)
                    dve.tensor_tensor(o_sb[1 - p][:, NFH:D], ps[:, 5, 0:D - NFH], x2b[1 - p][:, NFH:D], ALU.add) \
                       .then_inc(out_ready, 1)
                if has(i - 1):
                    dve.wait_ge(cx_ps, i)
                    dve.reciprocal(recip[:], cxp[:, :, :, HD]).then_inc(recip_ready, 1)
                    dve.wait_ge(recip_ready, i)
                    need(dve, cxt_ps, i - 1)
                    dve.tensor_tensor(cx[:].rearrange("p s h d -> p h s d"), cxp[:, :, :, 0:HD],
                                      recip[:].rearrange("p h (s d) -> p h s d", d=1).broadcast_to([P, KV, SPT, HD]),
                                      ALU.mult).then_inc(cx_ready, 1)
                if has(i):
                    dve.wait_ge(qkt_ps, i + 1)
                    need(dve, scores_ps, 2 * i)
                    dve.wait_ge(kt_hi, i + 1)
                    dve.tensor_tensor(kt_l[:], ps[:, 2, 0:P].rearrange("p (s t) -> p s t", s=SPT),
                                      kt_h[:].bitcast(F32), ALU.subtract).then_inc(kt_lo, 1)
                    dve.wait_ge(kt_lo, i + 1)
                    dve.tensor_tensor(k_bd_l[:], kt_l[:].rearrange("p s (h t) -> p s h t", h=1).broadcast_to([P, SPT, KV, T]),
                                      const("kvmask").rearrange("p (s h t) -> p s h t", s=1, t=1)
                                      .broadcast_to([P, SPT, KV, T]), ALU.mult).then_inc(k_bd_lo, 1)
                    dve.wait_ge(qt_hi, i + 1)
                    dve.tensor_tensor(qt_l[:].rearrange("p s (g t) -> p s g t", g=G),
                                      ps[:, 1, :].rearrange("p (g s t) -> p s g t", s=SPT, g=G),
                                      qt_h[:].bitcast(F32).rearrange("p s (g t) -> p s g t", g=G),
                                      ALU.subtract).then_inc(qt_lo, 1)
                if has(i - 1):
                    dve.wait_ge(cxt_hi, i)
                    dve.tensor_tensor(cxt_l[:].rearrange("p g s t -> p s g t"),
                                      ps[:, 0, :].rearrange("p (s g t) -> p s g t", s=SPT, g=G),
                                      cxt_h[:].bitcast(F32).rearrange("p g s t -> p s g t"), ALU.subtract).then_inc(cxt_lo, 1)
                if has(i - 2):
                    routing(i - 2)
                if has(i - 1):
                    dve.wait_ge(wo_ps, i)
                    dve.wait_ge(x_in[1 - p], k * 16 + 16 * p)
                    need(dve, x3t_ps, i - 1)
                    need(dve, x2b_ready, i - 1)
                    for n in range(0, D, D // 2):
                        dve.tensor_tensor(x2[:, n:n + D // 2], ps[:, 0, n:n + D // 2], x_nat[1 - p][:, n:n + D // 2],
                                          ALU.add).then_inc(x2_ready, 1)
                if has(i):
                    shift(i, 1)

            pipelined(dve, iteration)

        @block.tensor
        def _(pe):
            def product(out_ap, a_h, a_l, b_h, b_l, start, stop):
                pe.matmul(out_ap, a_h, b_h, start=start, stop=False)
                pe.matmul(out_ap, a_h, b_l, start=False, stop=False)
                return pe.matmul(out_ap, a_l, b_h, start=False, stop=stop)

            pe.wait_ge(set_up, 2)
            pe.matmul(ps[:, 0, 0:NA], const("before"), onehot[:], start=True, stop=True)
            pe.matmul(ps[:, 0, NA:2 * NA], const("ones"), onehot[:], start=True, stop=True).then_inc(route_ps, 1)
            pe.wait_ge(set_up, MATCH_STEP)
            pe.matmul(ps[0:1, 1, 0:NSLOT], const("sample"), match, start=True, stop=True).then_inc(route_ps, 1)
            for j in range(SPT):
                q = slice(j * T, (j + 1) * T)
                pe.matmul(ps[q, 2, 0:ST], const("sample_row"), match[:, j:NSLOT:SPT], start=True, stop=True)
                last = pe.matmul(ps[q, 2, ST:2 * ST], const("ones")[:, 0:T], match[:, j:NSLOT:SPT], start=True, stop=True)
            last.then_inc(route_ps, 1)
            for j in range(SPT):
                last = pe.matmul(ps[j * T:(j + 1) * T, 3, 0:NT], const("ones")[0:1, 0:T], idsm_f[0:1, j:NB:SPT],
                                 start=True, stop=True)
            last.then_inc(route_ps, 1)

            def adapters(i):
                return numbers(mybir.EngineType.PE, tile_adapter[0:1, bass.ds(i * XB, XB)], NA - 1)

            def adapter_product(i, u, a, again):
                pe.wait_ge(w_ready, a + 1)
                pe.wait_ge(xt_ready, i * XB + u + 1)
                if again:
                    pe.wait_ge(y_copied, i * XB + (u - XB + 1))
                for c in range(KC):
                    last = pe.matmul(ps[:, 4 + u, :], xt_sb[u % 2][:, c].rearrange("p s t -> p (s t)"),
                                     w_all[:, bass.ds(a, 1), c, :], start=(c == 0), stop=(c == KC - 1))
                last.then_inc(y_ps, 1)

            pe.wait_ge(routed, 2)
            for u, a in enumerate(adapters(0)):
                adapter_product(0, u, a, False)
            with pe.Fori(1, ST // XB) as i:
                for u, a in enumerate(adapters(i)):
                    adapter_product(i, u, a, True)

            pe.wait_ge(wqkv_lo, KC)
            pe.wait_ge(y_copied, ST)
            pe.wait_ge(mix_ready, SPT)

            def y_transpose(t, p, k):
                if has(t):
                    pe.wait_ge(y_in[p], k * 16 + 16)
                    need(pe, x2_ready, 2 * (t - 2))
                    for c in range(KC):
                        last = pe.transpose(ps[:, 0, c * P:(c + 1) * P], y_nat[p][:, c * P:(c + 1) * P], ident)
                    last.then_inc(yt_ps, 1)

            y_transpose(0, 0, 0)

            causal = causal_bf[:].rearrange("p (h t) -> p h t", h=1).broadcast_to([P, 2 * KV, T])

            def scores(half):
                if half == 0:
                    pe.matmul(ps[:, 3, :], ident_bf[:], causal, start=True, stop=False)
                for s in range(2 * half, 2 * half + 2):
                    n = (s % 2) * KV * T
                    last = product(ps[:, 3 + half, n:n + KV * T], qt_h[:, s, :], qt_l[:, s, :],
                                   k_bd_h[:, s].rearrange("p h t -> p (h t)"),
                                   k_bd_l[:, s].rearrange("p h t -> p (h t)"), half == 1, half == 1 or s == 1)
                return last

            def dense(c):
                for bank, n in ((7, 0), (5, NFH)):
                    last = product(ps[:, bank, 0:NFH], x3t_h[:, c, :], x3t_l[:, c, :],
                                   wf_h[:, c, n:n + NFH], wf_l[:, c, n:n + NFH], c == 0, c == KC - 1)
                return last

            def iteration(i, p, k):
                if has(i):
                    pe.wait_ge(yt_lo, i + 1)
                    need(pe, qt_lo, i)
                    need(pe, kt_lo, i)
                    for c in range(KC):
                        a_h, a_l = yt_h[:, c, :], yt_l[:, c, :]
                        product(ps[:, 1, :], a_h, a_l, wqkv_h[:, c, 0:NQ], wqkv_l[:, c, 0:NQ], c == 0, c == KC - 1)
                        last = product(ps[:, 2, 0:2 * NKV], a_h, a_l, wqkv_h[:, c, NQ:NQKV], wqkv_l[:, c, NQ:NQKV],
                                       c == 0, c == KC - 1)
                    last.then_inc(qkv_ps, 1)
                if has(i - 3):
                    pe.wait_ge(hw_ready, i - 2)
                    need(pe, x3t_lo, min(i - 1, NT) if isinstance(i, int) else i - 1)
                    pe.transpose(ps[:, 6, 0:P], hw[:].rearrange("p e r -> p (e r)"), ident).then_inc(hwt_ps, 1)
                if has(i - 1):
                    pe.wait_ge(exp_ready, 2 * i)
                    for h in range(KV):
                        n = (h % 4) * P
                        last = pe.transpose(ps[:, 3 + h // 4, n:n + P], prob[:, h].rearrange("p s t -> p (s t)"), ident)
                    last.then_inc(pt_ps, 1)
                y_transpose(i + 1, 1 - p, k + p if not isinstance(i, int) else (i + 1) // 2)
                if has(i - 3):
                    pe.wait_ge(hwt_ready, i - 2)
                    pe.matmul(ps[:, 7, 0:NFH], hwt[:], wb_sb[:, 0:NFH], start=False, stop=True, skip_group_check=True)
                    pe.matmul(ps[:, 5, 0:D - NFH], hwt[:], wb_sb[:, NFH:D], start=False, stop=True,
                              skip_group_check=True).then_inc(out_ps, 1)
                if has(i - 1):
                    pe.wait_ge(v_ready, i)
                    for h in range(KV):
                        if h % (KV // 2) == 0:
                            pe.wait_ge(pt_ready, 2 * i - 1 + h // (KV // 2))
                        n = (h % 4) * P
                        last = pe.matmul(ps[:, 3 + h // 4, n:n + SPT * VW], pt[:, h, :],
                                         v_bd[1 - p][:, h].rearrange("p s w -> p (s w)"), start=True, stop=True)
                    last.then_inc(cx_ps, 1)
                if has(i):
                    pe.wait_ge(roped, i + 1)
                    pe.wait_ge(v_ready, i + 1)
                    for g in range(G):
                        pe.transpose(ps[:, 1, g * P:(g + 1) * P], qk[:, g * P:(g + 1) * P], ident)
                    pe.transpose(ps[:, 2, 0:P], qk[:, NQ:NQK], ident).then_inc(qkt_ps, 1)
                if has(i - 2):
                    pe.wait_ge(x3t_lo, i - 1)
                    need(pe, out_ready, i - 2)
                    dense(0)
                if has(i - 1):
                    pe.wait_ge(cx_ready, i)
                    need(pe, yt_lo, min(i + 2, NT) if isinstance(i, int) else i + 2)
                    for s in range(SPT):
                        last = pe.transpose(ps[:, 0, s * P:(s + 1) * P], cx[:, s].rearrange("p h d -> p (h d)"), ident)
                    last.then_inc(cxt_ps, 1)
                if has(i - 2):
                    for c in range(1, KC):
                        last = dense(c)
                    last.then_inc(h_ps, 1)
                if isinstance(i, int) and i == 1:
                    pe.wait_ge(w2_lo, 1)
                if has(i - 1):
                    pe.wait_ge(cxt_lo, i)
                    for g in range(G):
                        last = product(ps[:, 0, :], cxt_h[:, g].rearrange("p s t -> p (s t)"),
                                       cxt_l[:, g].rearrange("p s t -> p (s t)"), wo_h[:, g, :], wo_l[:, g, :],
                                       g == 0, g == G - 1)
                    last.then_inc(wo_ps, 1)
                if has(i):
                    pe.wait_ge(qt_lo, i + 1)
                    pe.wait_ge(k_bd_lo, i + 1)
                    pe.wait_ge(k_bd_hi, i + 1)
                    for half in (1, 0):
                        scores(half).then_inc(scores_ps, 1)
                if has(i - 1):
                    need(pe, hwt_ready, i - 3)
                    mix = mix_bd[:, i - 1, :] if isinstance(i, int) else \
                        mix_bd[:, bass.ds(i - 1, 1), :].rearrange("p a n -> p (a n)")
                    for c in range(KC):
                        if c % (KC // 2) == 0:
                            pe.wait_ge(x2_ready, 2 * i - 1 + c // (KC // 2))
                        last = pe.matmul(ps[:, 6, c * P:(c + 1) * P], x2[:, c * P:(c + 1) * P], mix, start=True, stop=True)
                    last.then_inc(x3t_ps, 1)

            pipelined(pe, iteration)


MATCH_STEP = 11
WQKV_AT = 4
MIX_FROM = 6


def kernel(x, itok_B_1_14, itok_B_0_15, L0_cond_weight, L0_attn_Wq, L0_attn_Wk, L0_attn_Wv, L0_attn_Wo,
           L0_cond2_weights, L0_ffn_W_base, L0_ffn_b_base, L0_ffn_W_gate, L0_ffn_A, L0_ffn_B):
    import concourse.bacc as bacc
    from concourse.bass_utils import run_bass_kernel_spmd

    def chunked(w):
        return w.reshape(KC, P, w.shape[1]).transpose(1, 0, 2)

    a = np.asarray
    x = a(x)
    consts, where = constants()
    wq = a(L0_attn_Wq).reshape(D, KV, G, HD).transpose(0, 2, 1, 3).reshape(D, NQ)
    arrays = {
        "x": x.reshape(NB * T, D),
        "xt": x.reshape(NB, T, KC, P).transpose(0, 3, 2, 1).reshape(NB * P, KC * T),
        "ids_a": a(itok_B_1_14),
        "ids_m": a(itok_B_0_15),
        "wcond": a(L0_cond_weight).transpose(0, 2, 1).reshape(NA, KC, P, D).transpose(0, 2, 1, 3),
        "wqkv": chunked(np.concatenate([wq, a(L0_attn_Wk), a(L0_attn_Wv)], 1)),
        "wo": a(L0_attn_Wo).reshape(KV, G, HD, D).transpose(0, 2, 1, 3).reshape(P, G, D),
        "wmix": a(L0_cond2_weights).reshape(NA * T, T),
        "wffn": chunked(np.concatenate([a(L0_ffn_W_base).T, a(L0_ffn_A).reshape(ER, D).T, a(L0_ffn_W_gate).T], 1)),
        "wb": a(L0_ffn_B).transpose(0, 2, 1).reshape(ER, D),
        "bias": a(L0_ffn_b_base),
        "consts": consts,
    }
    arrays = {name: np.ascontiguousarray(v) for name, v in arrays.items()}
    nc = bacc.Bacc("TRN2", target_bir_lowering=False, num_devices=1)
    args = [nc.dram_tensor(name, v.shape, mybir.dt.from_np(v.dtype), kind="ExternalInput").ap()
            for name, v in arrays.items()]
    out = nc.dram_tensor("out", (NB * T, D), F32, kind="ExternalOutput").ap()
    build(nc, *args, out, where)
    result = run_bass_kernel_spmd(nc, [arrays], core_ids=[0])
    return result.results[0]["out"].reshape(NB, T, D)
```
